# Optimizing a Trainium2 kernel written in Bass

```python
import numpy as np
import jax
import jax.numpy as jnp

def _softmax(x, axis=-1):
    return jax.nn.softmax(x, axis=axis)

def _gelu(x):
    return jax.nn.gelu(x, approximate=True)

def _silu(x):
    return jax.nn.silu(x)

def _sigmoid(x):
    return jax.nn.sigmoid(x)

def _layernorm(x, axis=-1, eps=1e-05):
    m = jnp.mean(x, axis=axis, keepdims=True)
    v = jnp.var(x, axis=axis, keepdims=True)
    return (x - m) / jnp.sqrt(v + eps)

def _scatter_add(tgt, idx, src, axis=0):
    return tgt.at[idx].add(src)

def _segment_sum(src, seg, n):
    return jax.ops.segment_sum(src, seg, n)
kernel_name = 'mk_gnn_preln_d2_gnn_r8_7c30fe'

def setup_inputs(seed: int=0):
    np.random.seed(seed)
    _w = jnp.asarray

    def _rec_inputs():
        import jax
        import jax.numpy as jnp
        _gk = jax.random.key(seed)
        x = -0.0003713 + 1 * jax.random.normal(jax.random.fold_in(_gk, 1), (12500, 128), jnp.float32)
        src = jax.random.randint(jax.random.fold_in(_gk, 2), (200000,), 0, 12500, jnp.int32)
        dst = jax.random.randint(jax.random.fold_in(_gk, 3), (200000,), 0, 12500, jnp.int32)
        _o = jnp.argsort(dst, stable=True)
        src = src[_o]
        dst = dst[_o]
        edge_attr_128 = 5.93493e-05 + 1.00006 * jax.random.normal(jax.random.fold_in(_gk, 11), (200000, 128), jnp.float32)
        edge_attr_16 = -5.49627e-05 + 1.00015 * jax.random.normal(jax.random.fold_in(_gk, 12), (200000, 16), jnp.float32)
        edge_attr_24 = -0.000233973 + 0.999961 * jax.random.normal(jax.random.fold_in(_gk, 13), (200000, 24), jnp.float32)
        edge_attr_36 = 0.000243504 + 1.0001 * jax.random.normal(jax.random.fold_in(_gk, 14), (200000, 36), jnp.float32)
        return (x, src, dst, edge_attr_128, edge_attr_16, edge_attr_24, edge_attr_36)
    x, src, dst, edge_attr_128, edge_attr_16, edge_attr_24, edge_attr_36 = _rec_inputs()

    def _L0_gnn_setup():
        import jax, jax.numpy as jnp
        import numpy as np
        N_NODES = 12500
        N_EDGES = 75000
        D = 128
        key = jax.random.key(seed)
        ks = jax.random.split(key, 6)
        x = jax.random.normal(ks[0], (N_NODES, D), dtype=jnp.float32)
        edge_index = jax.random.randint(ks[1], (2, N_EDGES), 0, N_NODES, dtype=jnp.int64)
        edge_attr = jax.random.normal(ks[2], (N_EDGES, D), dtype=jnp.float32)
        scale = 1.0 / np.sqrt(3 * D)
        W_f = jax.random.normal(ks[3], (3 * D, D), dtype=jnp.float32) * scale
        b_f = jnp.zeros((D,), dtype=jnp.float32)
        W_s = jax.random.normal(ks[4], (3 * D, D), dtype=jnp.float32) * scale
        b_s = jnp.zeros((D,), dtype=jnp.float32)
        return {'x': x, 'edge_index': edge_index, 'edge_attr': edge_attr, 'W_f': W_f, 'b_f': b_f, 'W_s': W_s, 'b_s': b_s}
    _L0_gnn_all = _L0_gnn_setup()
    _L0_gnn_in = {k: v for k, v in _L0_gnn_all.items() if k in ('W_f', 'b_f', 'W_s', 'b_s')}
    del _L0_gnn_all

    def _L1_gnn_setup():
        import jax, jax.numpy as jnp
        import numpy as np
        N_NODES = 6250
        N_EDGES = 75000
        HID = 128
        MID = 64
        F0_IN = 24
        F1_IN = 36
        F2_IN = 16

        def _glorot(key, shape):
            fan_out, fan_in = shape
            s = jnp.sqrt(6.0 / (fan_in + fan_out))
            return jax.random.uniform(key, shape, jnp.float32, -s, s)

        def _linear(x, W, b=None):
            y = x @ W.T
            return y if b is None else y + b

        def _swish(x):
            return x * jax.nn.sigmoid(x)

        def _two_linear(x, Wa, Wb):
            return _linear(_linear(x, Wa), Wb)

        def _edge_conv(x, src, dst, ew, Wl, bl, Wr):
            msg = ew * x[src]
            agg = jax.ops.segment_sum(msg, dst, num_segments=x.shape[0])
            return _linear(agg, Wl, bl) + x @ Wr.T
        key = jax.random.key(seed)
        ks = jax.random.split(key, 40)
        it = iter(range(40))
        g = lambda shape: _glorot(ks[next(it)], shape)
        inp = {}
        inp['x'] = jax.random.normal(ks[next(it)], (N_NODES, HID), jnp.float32)
        inp['feature0'] = jax.random.normal(ks[next(it)], (N_EDGES, F0_IN), jnp.float32)
        inp['feature1'] = jax.random.normal(ks[next(it)], (N_EDGES, F1_IN), jnp.float32)
        inp['pos_emb'] = jax.random.normal(ks[next(it)], (N_EDGES, F2_IN), jnp.float32)
        inp['edge_index'] = jax.random.randint(ks[next(it)], (2, N_EDGES), 0, N_NODES)
        inp['W_lin_1'] = g((HID, HID))
        inp['b_lin_1'] = jnp.zeros((HID,), jnp.float32)
        inp['W_lin_2'] = g((HID, HID))
        inp['b_lin_2'] = jnp.zeros((HID,), jnp.float32)
        inp['Wf0a'] = g((MID, F0_IN))
        inp['Wf0b'] = g((HID, MID))
        inp['Wf1a'] = g((MID, F1_IN))
        inp['Wf1b'] = g((HID, MID))
        inp['Wf2a'] = g((MID, F2_IN))
        inp['Wf2b'] = g((HID, MID))
        for c in range(3):
            inp[f'Wl{c}'] = g((HID, HID))
            inp[f'bl{c}'] = jnp.zeros((HID,), jnp.float32)
            inp[f'Wr{c}'] = g((HID, HID))
            inp[f'Wo{c}'] = g((HID, HID))
            inp[f'bo{c}'] = jnp.zeros((HID,), jnp.float32)
        inp['W_lin3'] = g((HID, HID))
        inp['b_lin3'] = jnp.zeros((HID,), jnp.float32)
        return inp
    _L1_gnn_all = _L1_gnn_setup()
    _L1_gnn_in = {k: v for k, v in _L1_gnn_all.items() if k in ('W_lin_1', 'b_lin_1', 'W_lin_2', 'b_lin_2', 'Wf0a', 'Wf0b', 'Wf1a', 'Wf1b', 'Wf2a', 'Wf2b', 'Wl0', 'bl0', 'Wr0', 'Wo0', 'bo0', 'Wl1', 'bl1', 'Wr1', 'Wo1', 'bo1', 'Wl2', 'bl2', 'Wr2', 'Wo2', 'bo2', 'W_lin3', 'b_lin3')}
    del _L1_gnn_all
    return {'x': x, 'src': src, 'dst': dst, 'edge_attr_128': edge_attr_128, 'edge_attr_16': edge_attr_16, 'edge_attr_24': edge_attr_24, 'edge_attr_36': edge_attr_36, 'L0_gnn_W_f': _L0_gnn_in['W_f'], 'L0_gnn_b_f': _L0_gnn_in['b_f'], 'L0_gnn_W_s': _L0_gnn_in['W_s'], 'L0_gnn_b_s': _L0_gnn_in['b_s'], 'L1_gnn_W_lin_1': _L1_gnn_in['W_lin_1'], 'L1_gnn_b_lin_1': _L1_gnn_in['b_lin_1'], 'L1_gnn_W_lin_2': _L1_gnn_in['W_lin_2'], 'L1_gnn_b_lin_2': _L1_gnn_in['b_lin_2'], 'L1_gnn_Wf0a': _L1_gnn_in['Wf0a'], 'L1_gnn_Wf0b': _L1_gnn_in['Wf0b'], 'L1_gnn_Wf1a': _L1_gnn_in['Wf1a'], 'L1_gnn_Wf1b': _L1_gnn_in['Wf1b'], 'L1_gnn_Wf2a': _L1_gnn_in['Wf2a'], 'L1_gnn_Wf2b': _L1_gnn_in['Wf2b'], 'L1_gnn_Wl0': _L1_gnn_in['Wl0'], 'L1_gnn_bl0': _L1_gnn_in['bl0'], 'L1_gnn_Wr0': _L1_gnn_in['Wr0'], 'L1_gnn_Wo0': _L1_gnn_in['Wo0'], 'L1_gnn_bo0': _L1_gnn_in['bo0'], 'L1_gnn_Wl1': _L1_gnn_in['Wl1'], 'L1_gnn_bl1': _L1_gnn_in['bl1'], 'L1_gnn_Wr1': _L1_gnn_in['Wr1'], 'L1_gnn_Wo1': _L1_gnn_in['Wo1'], 'L1_gnn_bo1': _L1_gnn_in['bo1'], 'L1_gnn_Wl2': _L1_gnn_in['Wl2'], 'L1_gnn_bl2': _L1_gnn_in['bl2'], 'L1_gnn_Wr2': _L1_gnn_in['Wr2'], 'L1_gnn_Wo2': _L1_gnn_in['Wo2'], 'L1_gnn_bo2': _L1_gnn_in['bo2'], 'L1_gnn_W_lin3': _L1_gnn_in['W_lin3'], 'L1_gnn_b_lin3': _L1_gnn_in['b_lin3']}

def reference(x, src, dst, edge_attr_128, edge_attr_16, edge_attr_24, edge_attr_36, L0_gnn_W_f, L0_gnn_b_f, L0_gnn_W_s, L0_gnn_b_s, L1_gnn_W_lin_1, L1_gnn_b_lin_1, L1_gnn_W_lin_2, L1_gnn_b_lin_2, L1_gnn_Wf0a, L1_gnn_Wf0b, L1_gnn_Wf1a, L1_gnn_Wf1b, L1_gnn_Wf2a, L1_gnn_Wf2b, L1_gnn_Wl0, L1_gnn_bl0, L1_gnn_Wr0, L1_gnn_Wo0, L1_gnn_bo0, L1_gnn_Wl1, L1_gnn_bl1, L1_gnn_Wr1, L1_gnn_Wo1, L1_gnn_bo1, L1_gnn_Wl2, L1_gnn_bl2, L1_gnn_Wr2, L1_gnn_Wo2, L1_gnn_bo2, L1_gnn_W_lin3, L1_gnn_b_lin3):
    import jax
    import jax.numpy as jnp

    def _L0_gnn_ref(x, edge_index, edge_attr, W_f, b_f, W_s, b_s):
        import jax, jax.numpy as jnp
        import numpy as np
        N_NODES = 12500
        N_EDGES = 75000
        D = 128
        src = edge_index[0]
        dst = edge_index[1]
        z = jnp.concatenate([x[dst], x[src], edge_attr], axis=-1)
        gate = jax.nn.sigmoid(z @ W_f + b_f)
        val = jax.nn.softplus(z @ W_s + b_s)
        msg = gate * val
        agg = jax.ops.segment_sum(msg, dst, num_segments=N_NODES)
        return agg + x

    def _L1_gnn_ref(x, feature0, feature1, pos_emb, edge_index, W_lin_1, b_lin_1, W_lin_2, b_lin_2, Wf0a, Wf0b, Wf1a, Wf1b, Wf2a, Wf2b, Wl0, bl0, Wr0, Wo0, bo0, Wl1, bl1, Wr1, Wo1, bo1, Wl2, bl2, Wr2, Wo2, bo2, W_lin3, b_lin3):
        import jax, jax.numpy as jnp
        import numpy as np
        N_NODES = 6250
        N_EDGES = 75000
        HID = 128
        MID = 64
        F0_IN = 24
        F1_IN = 36
        F2_IN = 16

        def _glorot(key, shape):
            fan_out, fan_in = shape
            s = jnp.sqrt(6.0 / (fan_in + fan_out))
            return jax.random.uniform(key, shape, jnp.float32, -s, s)

        def _linear(x, W, b=None):
            y = x @ W.T
            return y if b is None else y + b

        def _swish(x):
            return x * jax.nn.sigmoid(x)

        def _two_linear(x, Wa, Wb):
            return _linear(_linear(x, Wa), Wb)

        def _edge_conv(x, src, dst, ew, Wl, bl, Wr):
            msg = ew * x[src]
            agg = jax.ops.segment_sum(msg, dst, num_segments=x.shape[0])
            return _linear(agg, Wl, bl) + x @ Wr.T
        src = edge_index[0]
        dst = edge_index[1]
        x_lin_1 = _swish(_linear(x, W_lin_1, b_lin_1))
        x_lin_2 = _swish(_linear(x, W_lin_2, b_lin_2))
        ew0 = _two_linear(feature0, Wf0a, Wf0b)
        h0 = _edge_conv(x_lin_1, src, dst, ew0, Wl0, bl0, Wr0)
        h0 = _swish(_linear(h0, Wo0, bo0))
        ew1 = _two_linear(feature1, Wf1a, Wf1b)
        h1 = _edge_conv(x_lin_1, src, dst, ew1, Wl1, bl1, Wr1)
        h1 = _swish(_linear(h1, Wo1, bo1))
        ew2 = _two_linear(pos_emb, Wf2a, Wf2b)
        h2 = _edge_conv(x_lin_2, src, dst, ew2, Wl2, bl2, Wr2)
        h2 = _swish(_linear(h2, Wo2, bo2))
        h = h0 + h1 + h2
        h = _swish(_linear(h, W_lin3, b_lin3))
        return h
    edge_index = jnp.stack([src, dst])
    h = jnp.maximum(_layernorm(x, axis=-1), 0.0)
    x = x + _L0_gnn_ref(h, edge_index, edge_attr_128, L0_gnn_W_f, L0_gnn_b_f, L0_gnn_W_s, L0_gnn_b_s)
    h = jnp.maximum(_layernorm(x, axis=-1), 0.0)
    x = x + _L1_gnn_ref(h, edge_attr_24, edge_attr_36, edge_attr_16, edge_index, L1_gnn_W_lin_1, L1_gnn_b_lin_1, L1_gnn_W_lin_2, L1_gnn_b_lin_2, L1_gnn_Wf0a, L1_gnn_Wf0b, L1_gnn_Wf1a, L1_gnn_Wf1b, L1_gnn_Wf2a, L1_gnn_Wf2b, L1_gnn_Wl0, L1_gnn_bl0, L1_gnn_Wr0, L1_gnn_Wo0, L1_gnn_bo0, L1_gnn_Wl1, L1_gnn_bl1, L1_gnn_Wr1, L1_gnn_Wo1, L1_gnn_bo1, L1_gnn_Wl2, L1_gnn_bl2, L1_gnn_Wr2, L1_gnn_Wo2, L1_gnn_bo2, L1_gnn_W_lin3, L1_gnn_b_lin3)
    return x

_drawn_inputs = setup_inputs


def setup_inputs(seed=0):
    import zlib

    import numpy as np

    out = dict(_drawn_inputs(seed))
    spreads = {'L0_gnn_b_f': (0.0, 0.1),
     'L0_gnn_b_s': (0.0, 0.1),
     'L1_gnn_b_lin_1': (0.0, 0.688),
     'L1_gnn_b_lin_2': (0.0, 0.8),
     'L1_gnn_bl0': (0.0, 0.8),
     'L1_gnn_bo0': (0.0, 0.8),
     'L1_gnn_bl1': (0.0, 0.8),
     'L1_gnn_bo1': (0.0, 0.8),
     'L1_gnn_bl2': (0.0, 0.8),
     'L1_gnn_bo2': (0.0, 0.8),
     'L1_gnn_b_lin3': (0.0, 0.8)}
    factors = {'L1_gnn_Wr0': 3.091, 'L1_gnn_Wr1': 3.043}
    for name, (base, spread) in spreads.items():
        noise = np.random.default_rng([zlib.crc32(name.encode()), seed]).standard_normal(out[name].shape)
        drawn = base * np.exp(spread * noise) if base else spread * noise
        out[name] = jnp.asarray(drawn.astype(out[name].dtype))
    for name, factor in factors.items():
        out[name] = (out[name] * factor).astype(out[name].dtype)
    return out
```

```python
import numpy as np
import concourse.bass as bass
import concourse.mybir as mybir
from concourse.alu_op_type import AluOpType as ALU
from contextlib import ExitStack

F32, BF16, I32 = mybir.dt.float32, mybir.dt.bfloat16, mybir.dt.int32
F32R = mybir.dt.float32r
ACT = mybir.ActivationFunctionType

D = 128
MID = 64
FEATS = (24, 36, 16)
FT = sum(FEATS)
TILE = 128
TPG = 4
GE = TILE * TPG
WIN = 40
PARTS = 3
WROWS = WIN * PARTS
NP = 125
NK = 4
NB = NP * NK
EPS = 1e-5
EXP_MAX = 80.0
DUP = -1.0e6
UNROLL = 4


def at(r, c):
    return c if r is None else r * UNROLL + c


def half(r, c):
    return c // 2 if r is None else r * (UNROLL // 2) + c // 2


def quarter(r, c):
    return c // UNROLL if r is None else r + c // UNROLL


def run(eng, n, least, step):
    head = min(n, least + (n - least) % UNROLL) if n > least else n
    for c in range(head):
        step(None, c)
    if n > head:
        with eng.Fori(0, (n - head) // UNROLL) as r:
            for u in range(UNROLL):
                step(r, head + u)


def run_skewed(eng, n, skew, step):
    head = skew + 2 + (n - skew - 2) % UNROLL
    for c in range(head):
        step(None, c)
    if n > head:
        with eng.Fori(0, (n - head) // UNROLL) as r:
            for u in range(UNROLL):
                step(r, head + u)
    for c in range(n, n + skew):
        step(None, c)


def address(eng, r, value):
    return value if r is None else eng.snap(value)


def group_rows(x, edge):
    return x[bass.ds(edge, GE), :].rearrange("(p j) d -> p j d", j=TPG)


class Sems:

    def __init__(self, nc, ctx, phase):
        self.nc, self.ctx, self.phase = nc, ctx, phase

    def one(self, name):
        return self.ctx.enter_context(self.nc.semaphore(f"{self.phase}_{name}"))

    def pair(self, name):
        return [self.one(f"{name}{i}") for i in range(2)]

    def four(self, name):
        return [self.one(f"{name}{i}") for i in range(4)]


def constants_and_weights(nc, T, S, P, N, E):
    G = -(-E // GE)
    BLK = 128
    full = G - 1
    nblk = -(-G // BLK)
    rows = [min(BLK, G - BLK * k) for k in range(nblk)]
    with ExitStack() as ctx:
        sem = Sems(nc, ctx, "pre")

        def sb(name, shape, dt=F32):
            return ctx.enter_context(nc.sbuf_tensor(f"pre_{name}", shape, dt))

        IW = 2 * nblk * GE
        idx_i = S["acc"][:, 0, 0:IW].bitcast(I32).rearrange("p (a k c) -> p a k c", a=2, k=nblk)
        idx_f = S["acc"][:, 1, 0:IW].rearrange("p (a k c) -> p a k c", a=2, k=nblk)
        far, far2 = (S["acc"][:, 2, n * nblk * GE:(n + 1) * nblk * GE].rearrange("p (k c) -> p k c", k=nblk) for n in range(2))
        rel16 = sb("rel16", [BLK, nblk, GE], BF16)
        dup = sb("dup", [BLK, GE])
        farsum = sb("farsum", [BLK, 1])
        wf = sb("wf", [D, 3, D])
        ws = sb("ws", [D, 3, D])
        w2 = sb("w2", [D, 2, D])
        wsq = sb("wsq", [D, 3, 3, D])
        w3 = sb("w3", [D, D])
        wa = [sb(f"wa{c}", [MID, FT]) for c in range(3)]
        wb = sb("wb", [D, 3, MID])
        wbT = sb("wbT", [MID, 3, D])
        woT = sb("woT", [D, 3, D])
        bl = sb("bl", [D, 3])
        bo = sb("bo", [D, 3])

        zeroed = sem.one("zeroed")
        idx_in = sem.one("idx_in")
        w_in = sem.one("w_in")
        idx_cast = sem.one("idx_cast")
        idx_rel = sem.one("idx_rel")
        rel_out = sem.one("rel_out")
        tr = sem.one("tr")
        tr_sb = sem.one("tr_sb")
        step_done = sem.one("step_done")
        far_sum = sem.one("far_sum")
        far_tot = sem.one("far_tot")
        wT = sem.one("wT")
        wT_sb = sem.one("wT_sb")
        fold = sem.one("fold")
        fold_sb = sem.one("fold_sb")
        neg = sem.one("neg")

        loads = []
        for part, x in enumerate((T["dst"], T["src"])):
            for k in range(nblk):
                n = min(rows[k], full - BLK * k)
                if n > 0:
                    loads.append((idx_i[0:n, part, k, :], x[BLK * k * GE:(BLK * k + n) * GE].rearrange("(p c) -> p c", c=GE)))
            k, p = full // BLK, full % BLK
            loads.append((idx_i[p:p + 1, part, k, :], x[E - GE:E].rearrange("(p c) -> p c", c=GE)))
        loads.append((S["base_i"][0:1, 0:full], T["dst"][0:full * GE].rearrange("(g c) -> g c", c=GE)[:, 0:1].rearrange("g c -> c g")))
        loads.append((S["base_i"][0:1, full:G], T["dst"][E - GE:E - GE + 1].rearrange("(p c) -> p c", c=1)))
        loads.append((dup[:, :], T["c_dup"]))
        wloads = [
            (S["ident"][:, :], T["c_ident"]), (S["iota"][:, :], T["c_iota"][0:WIN].partition_broadcast(128)),
            (S["wrow"][:, :], T["c_wrow"]),
            (wf[:, :, :], T["L0_gnn_W_f"].rearrange("(k p) n -> p k n", p=D)),
            (ws[:, :, :], T["L0_gnn_W_s"].rearrange("(k p) n -> p k n", p=D)),
            (S["bias_ab"][:, 0:D], T["L0_gnn_b_f"].partition_broadcast(NP)),
            (S["bias_ab"][:, D:2 * D], T["L0_gnn_b_s"].partition_broadcast(NP)),
            (S["bias_x"][:, 0:D], T["L1_gnn_b_lin_1"].partition_broadcast(NP)),
            (S["bias_x"][:, D:2 * D], T["L1_gnn_b_lin_2"].partition_broadcast(NP)),
            (w3[:, :], T["L1_gnn_W_lin3"]),
        ]
        column = lambda x: x.rearrange("(p c) -> p c", c=1)
        for n, x in enumerate(("L1_gnn_b_lin_1", "L1_gnn_b_lin_2", "L1_gnn_b_lin3")):
            wloads.append((S["bcol"][:, n:n + 1], column(T[x])))
        for n, x in enumerate(("L1_gnn_W_lin_1", "L1_gnn_W_lin_2")):
            wloads.append((w2[:, n, :], T[x]))
        start = [sum(FEATS[:c]) for c in range(3)]
        for c in range(3):
            for n, x in enumerate(("Wl", "Wr", "Wo")):
                wloads.append((wsq[:, c, n, :], T[f"L1_gnn_{x}{c}"]))
            wloads.append((wa[c][:, start[c]:start[c] + FEATS[c]], T[f"L1_gnn_Wf{c}a"]))
            wloads.append((wb[:, c, :], T[f"L1_gnn_Wf{c}b"]))
            wloads.append((bl[:, c:c + 1], column(T[f"L1_gnn_bl{c}"])))
            wloads.append((bo[:, c:c + 1], column(T[f"L1_gnn_bo{c}"])))
        NW = 16 * len(wloads)
        NI = 16 * len(loads)
        ident = S["ident"]
        flips = ([(w2[:, n, :], S["w_x"][:, n * D:(n + 1) * D], D) for n in range(2)]
                 + [(w3[:, :], S["w_out"][:, 6 * D:7 * D], D)]
                 + [(wsq[:, c, 2, :], woT[:, c, :], D) for c in range(3)]
                 + [(wb[:, c, :], wbT[:, c, :], MID) for c in range(3)])

        with nc.Block() as block:
            @block.sync
            def _(sp):
                sp.wait_ge(zeroed, 4 + nblk * 0)
                for o, i in loads:
                    sp.dma_start(o, i, allow_slow_non_contiguous=True).then_inc(idx_in, 16)
                sp.wait_ge(idx_rel, nblk + 3)
                for k in range(nblk):
                    sp.dma_start(T["rel_rows"][BLK * k:BLK * k + rows[k], :], rel16[0:rows[k], k, :]).then_inc(rel_out, 16)
                sp.wait_ge(fold_sb, 12)
                sp.dma_start(T["w_out"], S["w_out"][:, :]).then_inc(rel_out, 16)
                sp.wait_ge(rel_out, 16 * (nblk + 1))

            @block.scalar
            def _(act):
                act.wait_ge(zeroed, 4)
                for o, i in wloads:
                    act.dma_start(o, i, allow_slow_non_contiguous=True).then_inc(w_in, 16)

            @block.gpsimd
            def _(pool):
                nc.gpsimd.memset(idx_i[:, :, :, :], 0).then_inc(zeroed, 1)
                for c in range(3):
                    nc.gpsimd.memset(wa[c][:, :], 0.0).then_inc(zeroed, 1)

            @block.vector
            def _(dve):
                nc.vector.memset(S["ones"][:, :], 1.0).then_inc(step_done, 1)
                nc.vector.memset(S["eps"][:, :], EPS)
                dve.wait_ge(idx_in, NI)
                nc.vector.tensor_copy(idx_f[:, :, :, :], idx_i[:, :, :, :]).then_inc(idx_cast, 1)
                dve.wait_ge(idx_cast, 1)
                for k in range(nblk):
                    nc.vector.tensor_copy(S["base_f"][:, k:k + 1], idx_f[:, 0, k, 0:1]).then_inc(idx_cast, 1)
                dve.wait_ge(idx_cast, 1 + nblk)
                for k in range(nblk):
                    nc.vector.tensor_scalar(idx_f[:, 0, k, :], idx_f[:, 0, k, :], S["base_f"][:, k:k + 1], None, ALU.subtract).then_inc(idx_rel, 1)
                dve.wait_ge(idx_rel, nblk)
                nc.vector.tensor_scalar(far[:, :, :], idx_f[:, 0, :, :], float(WIN), None, ALU.is_ge).then_inc(step_done, 1)
                nc.vector.tensor_scalar(far2[:, :, :], idx_f[:, 0, :, :], 0.0, None, ALU.is_lt).then_inc(step_done, 1)
                dve.wait_ge(step_done, 3)
                nc.vector.scalar_tensor_tensor(out=idx_f[:, 0, nblk - 1, :], in0=dup[:, :], scalar=DUP, in1=idx_f[:, 0, nblk - 1, :],
                                               op0=ALU.mult, op1=ALU.add).then_inc(idx_rel, 1)
                nc.vector.tensor_tensor(far[:, :, :], far[:, :, :], far2[:, :, :], ALU.add).then_inc(step_done, 1)
                dve.wait_ge(step_done, 4)
                nc.vector.scalar_tensor_tensor(out=far2[:, 0, :], in0=dup[:, :], scalar=-1.0, in1=far[:, nblk - 1, :],
                                               op0=ALU.mult, op1=ALU.add).then_inc(step_done, 1)
                dve.wait_ge(step_done, 5)
                nc.vector.tensor_scalar(far[:, nblk - 1, :], far2[:, 0, :], 0.0, None, ALU.max).then_inc(step_done, 1)
                dve.wait_ge(idx_rel, nblk + 1)
                nc.vector.tensor_copy(rel16[:, :, :], idx_f[:, 0, :, :]).then_inc(idx_rel, 2)
                dve.wait_ge(step_done, 6)
                nc.vector.tensor_reduce(farsum[:, :], far[:, :, :].rearrange("p k c -> p (k c)"), mybir.AxisListType.X, ALU.add).then_inc(far_sum, 1)
                dve.wait_ge(w_in, NW)
                for k, o in ((0, S["w_ab"][:, 0:D]), (1, S["w_ab"][:, 2 * D:3 * D]), (2, S["w_e"][:, 0:D])):
                    nc.vector.tensor_scalar(o, wf[:, k, :], -1.0, None, ALU.mult).then_inc(neg, 1)
                for k, o in ((0, S["w_ab"][:, D:2 * D]), (1, S["w_ab"][:, 3 * D:4 * D]), (2, S["w_e"][:, D:2 * D])):
                    nc.vector.tensor_copy(o, ws[:, k, :]).then_inc(neg, 1)
                nc.vector.tensor_scalar(S["bias_ab"][:, 0:D], S["bias_ab"][:, 0:D], -1.0, None, ALU.mult).then_inc(neg, 1)
                for n in range(2 * nblk):
                    part, k = n % 2, n // 2
                    dve.wait_ge(tr, n + 1)
                    ps = P[:, n % 4, :].rearrange("p (j g) -> p g j", j=TPG)
                    out = (S["rel_t"], S["src_t"])[part]
                    nc.vector.tensor_copy(out[:, BLK * k:BLK * k + rows[k], :], ps[:, 0:rows[k], :]).then_inc(tr_sb, 1)
                dve.wait_ge(far_tot, 1)
                nc.vector.tensor_copy(S["far_i"][0:1, 0:1], P[0:1, 4, 0:1]).then_inc(far_sum, 1)
                for n, (_, o, m) in enumerate(flips):
                    dve.wait_ge(wT, n + 1)
                    nc.vector.tensor_copy(o, P[0:m, 5 + n % 2, 0:D]).then_inc(wT_sb, 1)
                for c in range(3):
                    dve.wait_ge(fold, c + 1)
                    ps = P[:, c, :]
                    nc.vector.tensor_copy(S["w_edge"][:, c * D:(c + 1) * D], ps[0:FT, 0:D]).then_inc(fold_sb, 1)
                    nc.vector.tensor_copy(S["w_out"][:, c * D:(c + 1) * D], ps[:, D:2 * D]).then_inc(fold_sb, 1)
                    nc.vector.tensor_copy(S["w_out"][:, (3 + c) * D:(4 + c) * D], ps[:, 2 * D:3 * D]).then_inc(fold_sb, 1)
                    nc.vector.tensor_tensor(S["b_h"][:, c:c + 1], ps[:, 3 * D:3 * D + 1], bo[:, c:c + 1], ALU.add).then_inc(fold_sb, 1)

            @block.tensor
            def _(pe):
                pe.wait_ge(w_in, NW)
                pe.wait_ge(idx_rel, nblk + 1)
                for n in range(2 * nblk):
                    part, k = n % 2, n // 2
                    if n >= 4:
                        pe.wait_ge(tr_sb, n - 3)
                    for j in range(TPG):
                        src = idx_f[0:rows[k], part, k, :].rearrange("g (p j) -> g j p", j=TPG)[:, j, :]
                        last = nc.tensor.transpose(P[:, n % 4, j * BLK:j * BLK + rows[k]], src, ident[0:rows[k], 0:rows[k]])
                    last.then_inc(tr, 1)
                pe.wait_ge(far_sum, 1)
                pe.wait_ge(step_done, 1)
                nc.tensor.matmul(P[0:1, 4, 0:1], farsum[:, 0:1], S["ones"][:, 0:1], start=True, stop=True).then_inc(far_tot, 1)
                for n, (i, _, m) in enumerate(flips):
                    if n >= 2:
                        pe.wait_ge(wT_sb, n - 1)
                    nc.tensor.transpose(P[0:m, 5 + n % 2, 0:D], i, ident[:, :]).then_inc(wT, 1)
                pe.wait_ge(wT_sb, len(flips))
                pe.wait_ge(tr_sb, 2 * nblk)
                for c in range(3):
                    ps = P[:, c, :]
                    nc.tensor.matmul(ps[0:FT, 0:D], wa[c][:, :], wbT[:, c, :], start=True, stop=True)
                    nc.tensor.matmul(ps[:, D:2 * D], wsq[:, c, 0, :], woT[:, c, :], start=True, stop=True)
                    nc.tensor.matmul(ps[:, 2 * D:3 * D], wsq[:, c, 1, :], woT[:, c, :], start=True, stop=True)
                    nc.tensor.matmul(ps[:, 3 * D:3 * D + 1], woT[:, c, :], bl[:, c:c + 1], start=True, stop=True).then_inc(fold, 1)


def norm_scales(nc, sem, stats, mean, rstd, tmp, eps, nt):
    chain = sem.one("ln_chain")
    var_ready = sem.one("ln_var")
    sqrt_ready = sem.one("ln_sqrt")
    m0, v0, m1, v1 = (stats[:, :, i:i + 1].rearrange("p t c -> p (t c)") for i in (1, 2, 4, 5))

    def vector(dve):
        def link(i, n):
            i.then_inc(chain, 1)
            dve.wait_ge(chain, n)
        link(nc.vector.tensor_tensor(mean[:, :], m0, m1, ALU.add), 1)
        link(nc.vector.tensor_tensor(tmp[:, 0, :], m0, m1, ALU.subtract), 2)
        link(nc.vector.tensor_scalar(mean[:, :], mean[:, :], 0.5, None, ALU.mult), 3)
        link(nc.vector.scalar_tensor_tensor(out=tmp[:, 0, :], in0=tmp[:, 0, :], scalar=0.25, in1=tmp[:, 0, :], op0=ALU.mult, op1=ALU.mult), 4)
        link(nc.vector.tensor_tensor(tmp[:, 1, :], v0, v1, ALU.add), 5)
        nc.vector.scalar_tensor_tensor(out=tmp[:, 0, :], in0=tmp[:, 1, :], scalar=1.0 / D, in1=tmp[:, 0, :], op0=ALU.mult, op1=ALU.add).then_inc(var_ready, 1)
        dve.wait_ge(sqrt_ready, 1)
        nc.vector.reciprocal(rstd[:, :], tmp[:, 1, :]).then_inc(chain, 1)
        dve.wait_ge(chain, 6)

    def scalar(act):
        act.wait_ge(var_ready, 1)
        nc.scalar.activation(tmp[:, 1, :], tmp[:, 0, :], ACT.Sqrt, bias=eps[0:NP, 0:1], scale=1.0).then_inc(sqrt_ready, 1)

    return vector, scalar


def node_tables(nc, T, S, P, N):
    NT = N // NB
    with ExitStack() as ctx:
        sem = Sems(nc, ctx, "nodes")

        def sb(name, shape, dt=F32):
            return ctx.enter_context(nc.sbuf_tensor(f"nodes_{name}", shape, dt))

        x = S["acc"][0:NP, 1, 0:NT * NK * D].rearrange("p (t d) -> p t d", d=D)
        stats = sb("stats", [NP, NT * NK, 6])
        mean, rstd = sb("mean", [NP, NT * NK]), sb("rstd", [NP, NT * NK])
        tmp = sb("tmp", [NP, 2, NT * NK])
        h = sb("h", [NP, 2, NK, D])
        hT = sb("hT", [D, 2, NB])
        room = S["acc"][0:NP, 2, :]
        a_f = room[:, 0:2 * 1024].rearrange("p (s k c) -> p s k c", s=2, k=NK)
        b_st = room[:, 2048:4096].rearrange("p (s k c) -> p s k c", s=2, k=NK)
        a_st = sb("a_st", [NP, 2, NK, PARTS, 2 * D], BF16)
        x_in, st_ready = sem.one("x_in"), sem.one("st_ready")
        h_ready, xh_ready = sem.one("h_ready"), sem.one("xh_ready")
        h_T, h_T_sb = sem.one("h_T"), sem.one("h_T_sb")
        ab, b_ready, af_ready = sem.one("ab"), sem.one("b_ready"), sem.one("af_ready")
        hi, mid_res, mid, lo = sem.one("hi"), sem.one("mid_res"), sem.one("mid"), sem.one("lo")
        a_out, b_out = sem.pair("a_out"), sem.pair("b_out")
        zero = sem.one("zero")
        norm_v, norm_s = norm_scales(nc, sem, stats, mean, rstd, tmp, S["eps"], NT * NK)
        LOADS = 5 if NT % 5 == 0 else 1
        XT = NT // LOADS
        ident = S["ident"]

        with nc.Block() as block:
            @block.sync
            def _(sp):
                for n in range(LOADS):
                    sp.dma_start(x[:, n * XT * NK:(n + 1) * XT * NK, :],
                                 T["x"][n * XT * NB:(n + 1) * XT * NB, :].rearrange("(t p) d -> p t d", p=NP)).then_inc(x_in, 16)

                def store(r, c):
                    s = c % 2
                    row = address(sp, r, at(r, c) * NB)
                    sp.wait_ge(b_ready, at(r, c + 1))
                    sp.dma_start(T["b_rows"][bass.ds(row, NB), :].rearrange("(k p) c -> p k c", p=NP), b_st[:, s]).then_inc(b_out[s], 16)
                    sp.wait_ge(lo, at(r, c + 1))
                    sp.dma_start(T["a_rows"][bass.ds(row, NB), :].rearrange("(k p) c -> p k c", p=NP),
                                 a_st[:, s].rearrange("p k a c -> p k (a c)")).then_inc(a_out[s], 16)
                run(sp, NT, 2, store)
                sp.wait_ge(zero, 1)
                sp.dma_start(T["a_rows"][N:N + WIN, :], a_st[0:WIN, 0, 0, :, :].rearrange("p a c -> p (a c)")).then_inc(a_out[0], 16)
                sp.wait_ge(a_out[0], 16 * ((NT + 1) // 2 + 1))
                sp.wait_ge(a_out[1], 16 * (NT // 2))
                sp.wait_ge(b_out[0], 16 * ((NT + 1) // 2))
                sp.wait_ge(b_out[1], 16 * (NT // 2))

            @block.vector
            def _(dve):
                nc.vector.memset(S["acc"][:, 0, :], 0.0)
                dve.wait_ge(x_in, 16 * LOADS)

                def st(r, c):
                    for k in range(NK):
                        t = at(r, c) * NK + k
                        last = nc.vector.bn_stats(stats[:, bass.ds(t, 1), :].rearrange("p t c -> p (t c)"),
                                                  x[:, bass.ds(t, 1), :].rearrange("p t c -> p (t c)"))
                    last.then_inc(st_ready, 1)
                run(dve, NT, 0, st)
                dve.wait_ge(st_ready, NT)
                norm_v(dve)

                def front(r, c):
                    s = c % 2
                    if c >= 2:
                        dve.wait_ge(h_T, at(r, c - 1))
                        dve.wait_ge(xh_ready, at(r, c - 1))
                    for k in range(NK):
                        t = at(r, c) * NK + k
                        last = nc.vector.tensor_scalar(h[:, s, k, :], x[:, bass.ds(t, 1), :].rearrange("p t c -> p (t c)"),
                                                       mean[:, bass.ds(t, 1)], rstd[:, bass.ds(t, 1)], ALU.subtract, ALU.mult)
                    last.then_inc(h_ready, 1)

                def xh(r, c):
                    xs = x[:, bass.ds(at(r, c) * NK, NK), :]
                    dve.wait_ge(h_ready, at(r, c + 1))
                    nc.vector.scalar_tensor_tensor(out=xs, in0=h[:, c % 2], scalar=0.0, in1=xs, op0=ALU.max, op1=ALU.add).then_inc(xh_ready, 1)

                def table(r, c):
                    s = c % 2
                    dve.wait_ge(ab, at(r, c + 1))
                    if c >= 2:
                        dve.wait_ge(lo, at(r, c - 1))
                    nc.vector.tensor_tensor(a_f[:, s], P[0:NP, 0:2, :].rearrange("p b (k c) -> p (b k) c", k=2),
                                            S["bias_ab"][:, :].unsqueeze(1).to_broadcast([NP, NK, 2 * D]), ALU.add).then_inc(af_ready, 1)

                def step(r, c):
                    if r is not None or c < NT:
                        front(r, c)
                        xh(r, c)
                    if r is not None or c >= 1:
                        table(r, c - 1)
                run_skewed(dve, NT, 1, step)
                dve.wait_ge(a_out[0], 16 * ((NT + 1) // 2))
                nc.vector.memset(a_st[:, 0, 0, :, :], 0.0).then_inc(zero, 1)

            @block.scalar
            def _(act):
                norm_s(act)

                def step(r, c):
                    s = c % 2
                    if r is not None or c < NT:
                        act.wait_ge(h_T, at(r, c + 1))
                        if c >= 2:
                            act.wait_ge(ab, at(r, c - 1))
                        nc.scalar.activation(hT[:, s, :], P[:, 4 + s, 0:NB], ACT.Relu).then_inc(h_T_sb, 1)
                    if r is not None or c >= 1:
                        g, s = c - 1, (c - 1) % 2
                        act.wait_ge(ab, at(r, g + 1))
                        if g >= 2:
                            act.wait_ge(b_out[s], half(r, g) * 16)
                            act.wait_ge(a_out[s], half(r, g) * 16)
                        nc.scalar.copy(b_st[:, s], P[0:NP, 2:4, :].rearrange("p b (k c) -> p (b k) c", k=2)).then_inc(b_ready, 1)
                        act.wait_ge(af_ready, at(r, g + 1))
                        nc.scalar.copy(a_st[:, s, :, 0, :], a_f[:, s]).then_inc(hi, 1)
                        act.wait_ge(mid_res, at(r, g + 1))
                        nc.scalar.copy(a_st[:, s, :, 1, :], a_f[:, s]).then_inc(mid, 1)
                run_skewed(act, NT, 1, step)

            @block.gpsimd
            def _(pool):
                def split(r, c):
                    s = c % 2
                    pool.wait_ge(hi, at(r, c + 1))
                    nc.gpsimd.tensor_tensor(a_f[:, s], a_f[:, s], a_st[:, s, :, 0, :], ALU.subtract).then_inc(mid_res, 1)
                    pool.wait_ge(mid, at(r, c + 1))
                    nc.gpsimd.tensor_tensor(a_st[:, s, :, 2, :], a_f[:, s], a_st[:, s, :, 1, :], ALU.subtract).then_inc(lo, 1)
                run(pool, NT, 2, split)

            @block.tensor
            def _(pe):
                def step(r, c):
                    s = c % 2
                    if r is not None or c < NT:
                        pe.wait_ge(h_ready, at(r, c + 1))
                        if c >= 2:
                            pe.wait_ge(h_T_sb, at(r, c - 1))
                        for k in range(NK):
                            last = nc.tensor.transpose(P[:, 4 + s, k * NP:(k + 1) * NP], h[:, s, k, :], ident[0:NP, 0:NP])
                        last.then_inc(h_T, 1)
                    if r is not None or c >= 1:
                        g, s = c - 1, (c - 1) % 2
                        pe.wait_ge(h_T_sb, at(r, g + 1))
                        if g >= 1:
                            pe.wait_ge(b_ready, at(r, g))
                            pe.wait_ge(af_ready, at(r, g))
                        for k in range(NK):
                            for a in range(2):
                                bank = P[0:NP, 2 * a + k // 2, (k % 2) * 2 * D:(k % 2 + 1) * 2 * D]
                                last = nc.tensor.matmul(bank, hT[:, s, k * NP:(k + 1) * NP], S["w_ab"][:, 2 * a * D:2 * (a + 1) * D], start=True, stop=True)
                        last.then_inc(ab, 1)
                run_skewed(pe, NT, 1, step)


def gated_edges(nc, T, S, P, N, E):
    G = -(-E // GE)
    with ExitStack() as ctx:
        sem = Sems(nc, ctx, "gate")

        def sb(name, shape, dt=F32):
            return ctx.enter_context(nc.sbuf_tensor(f"gate_{name}", shape, dt))

        acc = S["acc"][:, 0, :]
        room = S["acc"][:, 2, :]
        z = room[:, 0:2048].rearrange("p (s j c) -> p s j c", s=2, j=TPG)
        e = room[:, 2048:4096].rearrange("p (s j c) -> p s j c", s=2, j=TPG)
        rows = room[:, 4096:8192].rearrange("p (s j c) -> p s j c", s=4, j=TPG)
        msg = room[:, 8192:9216].rearrange("p (s j c) -> p s j c", s=2, j=TPG)
        ea = sb("ea", [128, 2, TPG, D])
        eaT = sb("eaT", [128, 2, TPG, TILE])
        win = sb("win", [WROWS, 2, 2 * D], BF16)
        relb = sb("relb", [WROWS, 2, GE], BF16)
        ohT = sb("ohT", [WROWS, 2, GE], BF16)
        oh = sb("oh", [128, 2, TPG, WIN])
        idx = sb("idx", [128, 4, TPG], I32)
        wsum = sb("wsum", [WIN, D])
        ea_in, win_in, relb_in = (sem.pair(x) for x in ("ea_in", "win_in", "relb_in"))
        rows_in = sem.four("rows_in")
        gathers_begun = sem.one("gathers_begun")
        idx_ready, ea_T, ea_T_sb = sem.one("idx_ready"), sem.one("ea_T"), sem.one("ea_T_sb")
        ohT_ready, oh_ready, z_psum, z_sum = sem.one("ohT_ready"), sem.one("oh_ready"), sem.one("z_psum"), sem.one("z_sum")
        clamped, exp_done, ln_done, gate = sem.one("clamped"), sem.one("exp_done"), sem.one("ln_done"), sem.one("gate")
        val, msg_ready, added = sem.one("val"), sem.one("msg_ready"), sem.one("added")
        sums, sums_sb, sums_T = sem.one("sums"), sem.one("sums_sb"), sem.one("sums_T")
        ident = S["ident"]

        def first_edge(eng, r, c):
            return E - GE if r is None and c == G - 1 else address(eng, r, at(r, c) * GE)

        def live(r, c):
            return r is not None or 0 <= c < G

        with nc.Block() as block:
            @block.sync
            def _(sp):
                def load(r, c):
                    s = c % 2
                    edge = first_edge(sp, r, c)
                    group = address(sp, r, at(r, c))
                    rel_row = address(sp, r, at(r, c) * GE)
                    base = sp.value_load(S["base_i"][0:1, bass.ds(group, 1)], min_val=0, max_val=N - 1)
                    window = address(sp, 0, base * PARTS)
                    if c >= 2:
                        sp.wait_ge(ea_T, at(r, c - 1))
                    sp.dma_start(ea[:, s], group_rows(T["edge_attr_128"], edge)).then_inc(ea_in[s], 16)
                    if c >= 2:
                        sp.wait_ge(ohT_ready, at(r, c - 1))
                        sp.wait_ge(z_psum, at(r, c - 1))
                    sp.dma_start(win[:, s, :], T["a_rows"].rearrange("n (a c) -> (n a) c", a=PARTS)[bass.ds(window, WROWS), :]).then_inc(win_in[s], 16)
                    sp.dma_start(relb[:, s, :], T["rel_rows"].rearrange("g c -> (g c)")[bass.ds(rel_row, GE)].partition_broadcast(WROWS)).then_inc(relb_in[s], 16)
                run(sp, G - 1, 2, load)
                load(None, G - 1)

            @block.gpsimd
            def _(pool):
                def gather(r, c):
                    s = c % 4
                    if c == 0 or c % 2 == G % 2:
                        pool.wait_ge(idx_ready, at(r, 1 if c == 0 and G % 2 else c + 2))
                        if c >= 3:
                            pool.wait_ge(z_sum, at(r, c - 2))
                        pool.sem_inc(gathers_begun, 1)
                    for j in range(TPG):
                        nc.gpsimd.indirect_dma_start(rows[:, s, j, :], None, T["b_rows"],
                                                     bass.IndirectOffsetOnAxis(ap=idx[:, c % 4, j:j + 1], axis=0)).then_inc(rows_in[s], 16)
                run(pool, G, 4, gather)

            @block.scalar
            def _(act):
                nc.scalar.preload_act_table_set("natural_log_exp_and_others")

                def indices(r, c):
                    if c >= 4:
                        act.wait_ge(z_sum, at(r, c - 3))
                    nc.scalar.copy(idx[:, c % 4, :], S["src_t"][:, bass.ds(at(r, c), 1), :].rearrange("p g j -> p (g j)")).then_inc(idx_ready, 1)
                indices(None, 0)
                indices(None, 1)

                def step(r, c):
                    if (r is None and c + 2 < G) or (r is not None):
                        indices(r, c + 2)
                    if live(r, c):
                        s = c % 2
                        act.wait_ge(ea_T, at(r, c + 1))
                        if c >= 2:
                            act.wait_ge(z_psum, at(r, c - 1))
                        nc.scalar.copy(eaT[:, s], P[:, 4 + s, :].rearrange("p (j e) -> p j e", j=TPG)).then_inc(ea_T_sb, 1)
                    if live(r, c - 1):
                        s = (c - 1) % 2
                        act.wait_ge(clamped, at(r, c))
                        nc.scalar.activation(e[:, s], e[:, s], ACT.Exp).then_inc(exp_done, 1)
                    if live(r, c - 3):
                        g = c - 3
                        act.wait_ge(sums, at(r, g + 1))
                        if g >= 1:
                            act.wait_ge(sums_T, at(r, g))
                        nc.scalar.copy(wsum[:, :], P[0:WIN, 6, 0:D]).then_inc(sums_sb, 1)
                    if live(r, c - 1):
                        s = (c - 1) % 2
                        act.wait_ge(exp_done, at(r, c))
                        nc.scalar.activation(e[:, s], e[:, s], ACT.Ln, bias=1.0).then_inc(ln_done, 1)
                        act.wait_ge(ln_done, at(r, c))
                        nc.scalar.activation(e[:, s, :, 0:D], e[:, s, :, 0:D], ACT.Exp, scale=-1.0).then_inc(gate, 1)
                run_ahead(act, G, 5, 2, step)

            @block.vector
            def _(dve):
                def step(r, c):
                    if live(r, c - 5):
                        g = c - 5
                        base = dve.value_load(S["base_i"][0:1, bass.ds(at(r, g), 1)], min_val=0, max_val=N - 1)
                        dve.wait_ge(sums_T, at(r, g + 1))
                        if g >= 1:
                            dve.wait_ge(added, at(r, g))
                        nc.vector.tensor_tensor(acc[:, bass.ds(base, WIN)], acc[:, bass.ds(base, WIN)], P[:, 7, 0:WIN], ALU.add).then_inc(added, 1)
                    if live(r, c):
                        s = c % 2
                        dve.wait_ge(relb_in[s], (half(r, c) + 1) * 16)
                        if c >= 2:
                            dve.wait_ge(z_psum, at(r, c - 1))
                        nc.vector.tensor_scalar(ohT[:, s, :], relb[:, s, :], S["wrow"][:, 0:1], None, ALU.is_equal).then_inc(ohT_ready, 1)
                    if live(r, c - 1):
                        g, s = c - 1, (c - 1) % 2
                        dve.wait_ge(z_psum, at(r, g + 1))
                        dve.wait_ge(rows_in[g % 4], (quarter(r, g) + 1) * 16 * TPG)
                        if g >= 2:
                            dve.wait_ge(val, at(r, g - 1))
                        nc.vector.tensor_tensor(z[:, s], P[:, 2 * s:2 * s + 2, :].rearrange("p b (j c) -> p (b j) c", j=2), rows[:, g % 4], ALU.add).then_inc(z_sum, 1)
                        dve.wait_ge(z_sum, at(r, g + 1))
                        if g >= 2:
                            dve.wait_ge(msg_ready, at(r, g - 1))
                        nc.vector.tensor_scalar(e[:, s], z[:, s], EXP_MAX, None, ALU.min).then_inc(clamped, 1)
                    if live(r, c - 2):
                        g, s = c - 2, c % 2
                        if g >= 2:
                            dve.wait_ge(sums, at(r, g - 1))
                        nc.vector.tensor_tensor(oh[:, s], S["iota"][:, 0:WIN].unsqueeze(1).to_broadcast([128, TPG, WIN]),
                                                S["rel_t"][:, bass.ds(at(r, g), 1), :].rearrange("p g j -> p (g j)").unsqueeze(2).to_broadcast([128, TPG, WIN]),
                                                ALU.is_equal).then_inc(oh_ready, 1)
                        dve.wait_ge(ln_done, at(r, g + 1))
                        nc.vector.tensor_tensor(e[:, s, :, D:2 * D], e[:, s, :, D:2 * D], z[:, s, :, D:2 * D], ALU.max).then_inc(val, 1)
                        dve.wait_ge(val, at(r, g + 1))
                        dve.wait_ge(gate, at(r, g + 1))
                        nc.vector.tensor_tensor(msg[:, s], e[:, s, :, 0:D], e[:, s, :, D:2 * D], ALU.mult).then_inc(msg_ready, 1)
                run_skewed(dve, G, 5, step)

            @block.tensor
            def _(pe):
                def step(r, c):
                    if live(r, c):
                        s = c % 2
                        pe.wait_ge(ea_in[s], (half(r, c) + 1) * 16)
                        if c >= 2:
                            pe.wait_ge(ea_T_sb, at(r, c - 1))
                        for j in range(TPG):
                            last = nc.tensor.transpose(P[:, 4 + s, j * TILE:(j + 1) * TILE], ea[:, s, j, :], ident[:, :])
                        last.then_inc(ea_T, 1)
                    if live(r, c - 1):
                        g, s = c - 1, (c - 1) % 2
                        pe.wait_ge(ea_T_sb, at(r, g + 1))
                        pe.wait_ge(win_in[s], (half(r, g) + 1) * 16)
                        pe.wait_ge(ohT_ready, at(r, g + 1))
                        if g >= 2:
                            pe.wait_ge(z_sum, at(r, g - 1))
                        tile_oh = ohT[:, s, :].rearrange("w (p j) -> w j p", j=TPG)
                        for j in range(TPG):
                            zp = P[:, 2 * s + j // 2, (j % 2) * 2 * D:(j % 2 + 1) * 2 * D]
                            nc.tensor.matmul(zp, eaT[:, s, j, :], S["w_e"][:, :], start=True, stop=False)
                            last = nc.tensor.matmul(zp, tile_oh[:, j, :], win[:, s, :], start=False, stop=True)
                        last.then_inc(z_psum, 1)
                    if live(r, c - 4):
                        g = c - 4
                        pe.wait_ge(sums_sb, at(r, g + 1))
                        if g >= 1:
                            pe.wait_ge(added, at(r, g))
                    if live(r, c - 3):
                        g, s = c - 3, (c - 3) % 2
                        pe.wait_ge(msg_ready, at(r, g + 1))
                        pe.wait_ge(oh_ready, at(r, g + 1))
                        if g >= 1:
                            pe.wait_ge(sums_sb, at(r, g))
                        for j in range(TPG):
                            last = nc.tensor.matmul(P[0:WIN, 6, 0:D], oh[:, s, j, :], msg[:, s, j, :], start=j == 0, stop=j == TPG - 1)
                        last.then_inc(sums, 1)
                    if live(r, c - 4):
                        nc.tensor.transpose(P[:, 7, 0:WIN], wsum[:, :], ident[0:WIN, 0:WIN]).then_inc(sums_T, 1)
                run_skewed(pe, G, 5, step)


def run_ahead(eng, n, skew, ahead, step):
    head = skew + 2 + (n - ahead - skew - 2) % UNROLL
    for c in range(head):
        step(None, c)
    if n - ahead > head:
        with eng.Fori(0, (n - ahead - head) // UNROLL) as r:
            for u in range(UNROLL):
                step(r, head + u)
    for c in range(n - ahead, n + skew):
        step(None, c)


def far_edges(nc, T, S, P, N, E, layer):
    G, NT = -(-E // GE), N // NB
    FAR = 1.0e6
    accs = 1 if layer == 0 else 3
    with ExitStack() as ctx:
        sem = Sems(nc, ctx, f"far{layer}")
        room = [0]

        def sb(name, shape, dt=F32):
            if layer == 1:
                return ctx.enter_context(nc.sbuf_tensor(f"far_{name}", [128] + shape, dt))[:]
            n = int(np.prod(shape)) // (2 if dt == BF16 else 1)
            flat = S["acc"][:, 2, room[0]:room[0] + n]
            room[0] += n
            names = "abc"[:len(shape)]
            flat = flat if dt == F32 else flat.bitcast(dt)
            return flat.rearrange(f"p ({' '.join(names)}) -> p {' '.join(names)}", **dict(zip(names, shape)))

        rows = sb("rows", [TPG, 2 * D])
        msg = sb("msg", [TPG, accs * D])
        oh = sb("oh", [TPG, NB])
        iota = sb("iota", [NB])
        dst_i, src_i = sb("dst_i", [TPG], I32), sb("src_i", [TPG], I32)
        dst_f, near, mark = sb("dst_f", [TPG]), sb("near", [TPG]), sb("mark", [TPG])
        if layer == 0:
            z, e = sb("z", [TPG, 2 * D]), sb("e", [TPG, 2 * D])
            parts = sb("parts", [TPG, PARTS * 2 * D], BF16)
            ea, eaT = sb("ea", [TPG, D]), sb("eaT", [TPG, TILE])
            streams = ((ea, T["edge_attr_128"]),)
        else:
            raw = [sb(f"raw{c}", [TPG, FEATS[c]]) for c in range(3)]
            f, fT = sb("f", [TPG, FT]), sb("fT", [TPG, TILE])
            streams = tuple(zip(raw, (T["edge_attr_24"], T["edge_attr_36"], T["edge_attr_16"])))
        start = [sum(FEATS[:c]) for c in range(3)]
        LOADS = len(streams) + 2
        GATHERS = TPG * (2 if layer == 0 else 1)
        iota_in, free, loaded, begun, gathered = (sem.one(x) for x in ("iota_in", "free", "loaded", "begun", "gathered"))
        repacked, flipped, flipped_sb, product = (sem.one(x) for x in ("repacked", "flipped", "flipped_sb", "product"))
        clamped, act_chain, chain, oh_ready, shifted, sums, added = (sem.one(x) for x in ("clamped", "act_chain", "chain", "oh_ready", "shifted", "sums", "added"))
        ident = S["ident"]

        def if_any(eng, body):
            left = eng.value_load(S["far_i"][0:1, 0:1], min_val=0, max_val=E)
            with eng.If(left > 0):
                if G > 1:
                    with eng.Fori(0, G - 1) as g:
                        body(g, g * GE)
                body(G - 1, E - GE)

        with nc.Block() as block:
            @block.sync
            def _(sp):
                sp.dma_start(iota, T["c_iota"].partition_broadcast(128)).then_inc(iota_in, 16)
                sp.wait_ge(iota_in, 16)

                def load(g, edge):
                    edge = edge if type(edge) is int else sp.snap(edge)
                    row = edge if type(edge) is int else sp.snap(edge * 1)
                    sp.wait_ge(free, g + 1)
                    for to, of in streams:
                        sp.dma_start(to, group_rows(of, edge)).then_inc(loaded, 16)
                    for to, of in ((dst_i, T["dst"]), (src_i, T["src"])):
                        sp.dma_start(to, of[bass.ds(row, GE)].rearrange("(p j) -> p j", j=TPG)).then_inc(loaded, 16)
                if_any(sp, load)

            @block.gpsimd
            def _(pool):
                def gather(g, edge):
                    pool.wait_ge(loaded, g * 16 * LOADS + 16 * LOADS)
                    pool.sem_inc(begun, 1)
                    for j in range(TPG):
                        by_src = bass.IndirectOffsetOnAxis(ap=src_i[:, j:j + 1], axis=0)
                        by_dst = bass.IndirectOffsetOnAxis(ap=dst_i[:, j:j + 1], axis=0)
                        nc.gpsimd.indirect_dma_start(rows[:, j, :], None, T["b_rows" if layer == 0 else "x_rows"], by_src).then_inc(gathered, 16)
                        if layer == 0:
                            nc.gpsimd.indirect_dma_start(parts[:, j, :], None, T["a_rows"], by_dst).then_inc(gathered, 16)
                if_any(pool, gather)

            @block.scalar
            def _(act):
                def messages(g, edge):
                    if layer == 0:
                        act.wait_ge(flipped, g + 1)
                        nc.scalar.copy(eaT, P[:, 4, :].rearrange("p (j e) -> p j e", j=TPG)).then_inc(flipped_sb, 1)
                        act.wait_ge(clamped, g + 1)
                        nc.scalar.activation(e, e, ACT.Exp).then_inc(act_chain, 1)
                        act.wait_ge(act_chain, g * 3 + 1)
                        nc.scalar.activation(e, e, ACT.Ln, bias=1.0).then_inc(act_chain, 1)
                        act.wait_ge(act_chain, g * 3 + 2)
                        nc.scalar.activation(e[:, :, 0:D], e[:, :, 0:D], ACT.Exp, scale=-1.0).then_inc(act_chain, 1)
                    else:
                        act.wait_ge(loaded, g * 16 * LOADS + 16 * LOADS)
                        for n in range(3):
                            last = nc.scalar.copy(f[:, :, start[n]:start[n] + FEATS[n]], raw[n])
                        last.then_inc(repacked, 1)
                        act.wait_ge(flipped, g + 1)
                        nc.scalar.copy(fT[0:FT], P[0:FT, 4, :].rearrange("p (j e) -> p j e", j=TPG)).then_inc(flipped_sb, 1)
                if_any(act, messages)

            @block.tensor
            def _(pe):
                def products(g, edge):
                    if layer == 0:
                        pe.wait_ge(loaded, g * 16 * LOADS + 16 * LOADS)
                        for j in range(TPG):
                            last = nc.tensor.transpose(P[:, 4, j * TILE:(j + 1) * TILE], ea[:, j, :], ident[:, :])
                        last.then_inc(flipped, 1)
                        pe.wait_ge(flipped_sb, g + 1)
                        for j in range(TPG):
                            last = nc.tensor.matmul(P[:, j // 2, (j % 2) * 2 * D:(j % 2 + 1) * 2 * D], eaT[:, j, :], S["w_e"][:, :], start=True, stop=True)
                        last.then_inc(product, 1)
                    else:
                        pe.wait_ge(repacked, g + 1)
                        for j in range(TPG):
                            last = nc.tensor.transpose(P[0:FT, 4, j * TILE:(j + 1) * TILE], f[:, j, :], ident[:, :])
                        last.then_inc(flipped, 1)
                        pe.wait_ge(flipped_sb, g + 1)
                        for j in range(TPG):
                            last = nc.tensor.matmul(P[:, j, 0:3 * D], fT[0:FT, j, :], S["w_edge"][:, :], start=True, stop=True)
                        last.then_inc(product, 1)
                    with pe.Fori(0, NT) as b:
                        pe.wait_ge(oh_ready, g * NT + b + 1)
                        for a in range(accs):
                            for j in range(TPG):
                                last = nc.tensor.matmul(P[:, 5 + a, 0:NB], msg[:, j, a * D:(a + 1) * D], oh[:, j, :], start=j == 0, stop=j == TPG - 1)
                        last.then_inc(sums, 1)
                if_any(pe, products)

            @block.vector
            def _(dve):
                dve.wait_ge(iota_in, 16)
                dve.sem_inc(free, 1)

                def spread(g, edge):
                    done = [0]
                    LINKS = 11 if layer == 0 else 6

                    def link(i):
                        done[0] += 1
                        i.then_inc(chain, 1)
                        dve.wait_ge(chain, g * LINKS + done[0])
                    dve.wait_ge(loaded, g * 16 * LOADS + 16 * LOADS)
                    rel = S["rel_t"][:, bass.ds(g, 1), :].rearrange("p g j -> p (g j)")
                    link(nc.vector.tensor_scalar(near, rel, 0.0, None, ALU.is_ge))
                    link(nc.vector.tensor_scalar(mark, rel, float(WIN), None, ALU.is_lt))
                    link(nc.vector.tensor_tensor(near, near, mark, ALU.mult))
                    link(nc.vector.scalar_tensor_tensor(out=near, in0=rel, scalar=DUP / 2, in1=near, op0=ALU.is_lt, op1=ALU.add))
                    link(nc.vector.tensor_copy(dst_f, dst_i))
                    link(nc.vector.scalar_tensor_tensor(out=dst_f, in0=near, scalar=FAR, in1=dst_f, op0=ALU.mult, op1=ALU.add))
                    dve.wait_ge(product, g + 1)
                    dve.wait_ge(gathered, g * 16 * GATHERS + 16 * GATHERS)
                    if layer == 0:
                        link(nc.vector.tensor_tensor(z, P[:, 0:2, :].rearrange("p b (j c) -> p (b j) c", j=2), rows, ALU.add))
                        for n in range(PARTS):
                            link(nc.vector.tensor_tensor(z, z, parts[:, :, n * 2 * D:(n + 1) * 2 * D], ALU.add))
                        nc.vector.tensor_scalar(e, z, EXP_MAX, None, ALU.min).then_inc(clamped, 1)
                        dve.wait_ge(act_chain, g * 3 + 3)
                        link(nc.vector.tensor_tensor(e[:, :, D:2 * D], e[:, :, D:2 * D], z[:, :, D:2 * D], ALU.max))
                        nc.vector.tensor_tensor(msg, e[:, :, 0:D], e[:, :, D:2 * D], ALU.mult)
                    else:
                        for j in range(TPG):
                            nc.vector.tensor_tensor(msg[:, j, 0:2 * D].rearrange("p (a d) -> p a d", a=2), P[:, j, 0:2 * D].rearrange("p (a d) -> p a d", a=2),
                                                    rows[:, j, 0:D].unsqueeze(1).to_broadcast([128, 2, D]), ALU.mult)
                            nc.vector.tensor_tensor(msg[:, j, 2 * D:3 * D], P[:, j, 2 * D:3 * D], rows[:, j, D:2 * D], ALU.mult)
                    with dve.Fori(0, NT) as b:
                        for j in range(TPG):
                            last = nc.vector.tensor_scalar(oh[:, j, :], iota, dst_f[:, j:j + 1], None, ALU.is_equal)
                        last.then_inc(oh_ready, 1)
                        dve.wait_ge(oh_ready, g * NT + b + 1)
                        nc.vector.tensor_scalar(dst_f, dst_f, -float(NB), None, ALU.add).then_inc(shifted, 1)
                        dve.wait_ge(sums, g * NT + b + 1)
                        dve.wait_ge(shifted, g * NT + b + 1)
                        block_acc = S["acc"][:, 0:accs, bass.ds(b * NB, NB)]
                        nc.vector.tensor_tensor(block_acc, block_acc, P[:, 5:5 + accs, 0:NB], ALU.add).then_inc(added, 1)
                        dve.wait_ge(added, g * NT + b + 1)
                    dve.sem_inc(free, 1)
                if_any(dve, spread)


def node_update(nc, T, S, P, N):
    NT = N // NB
    with ExitStack() as ctx:
        sem = Sems(nc, ctx, "upd")

        def sb(name, shape, dt=F32):
            return ctx.enter_context(nc.sbuf_tensor(f"upd_{name}", shape, dt))

        acc = S["acc"][:, 0, :]
        x = S["acc"][0:NP, 1, 0:NT * NK * D].rearrange("p (t d) -> p t d", d=D)
        stats = sb("stats", [NP, NT * NK, 6])
        mean, rstd = sb("mean", [NP, NT * NK]), sb("rstd", [NP, NT * NK])
        tmp = sb("tmp", [NP, 2, NT * NK])
        ag = sb("ag", [D, 2, NB])
        h = sb("h", [NP, 2, NK, D])
        hT = sb("hT", [D, 2, NB])
        room = S["acc"][:, 2, :]
        rows = room[0:NP, 0:2048].rearrange("p (s k c) -> p s k c", s=2, k=NK)
        pre = room[0:NP, 2048:4096].rearrange("p (s k c) -> p s k c", s=2, k=NK)
        cols = room[:, 4096:4096 + 4 * NB].rearrange("p (s a c) -> p s a c", s=2, a=2)
        ag_sb, ag_T, x1_ready, st_ready = sem.one("ag_sb"), sem.one("ag_T"), sem.one("x1_ready"), sem.one("st_ready")
        x1_out, h_ready, h_T, h_T_sb = sem.one("x1_out"), sem.one("h_ready"), sem.one("h_T"), sem.one("h_T_sb")
        lin_rows, lin_cols, pre_ready = sem.one("lin_rows"), sem.one("lin_cols"), sem.one("pre_ready")
        rows_ready, cols_ready = sem.one("rows_ready"), sem.one("cols_ready")
        rows_out, cols_out = sem.pair("rows_out"), sem.pair("cols_out")
        norm_v, norm_s = norm_scales(nc, sem, stats, mean, rstd, tmp, S["eps"], NT * NK)
        ident = S["ident"]

        with nc.Block() as block:
            @block.sync
            def _(sp):
                sp.wait_ge(x1_ready, NT)
                sp.dma_start(T["x1"].rearrange("(t p) d -> p t d", p=NP), x).then_inc(x1_out, 16)

                def store(r, c):
                    s = c % 2
                    row = address(sp, r, at(r, c) * NB)
                    col = address(sp, r, at(r, c) * 2 * NB)
                    sp.wait_ge(rows_ready, at(r, c + 1))
                    sp.dma_start(T["x_rows"][bass.ds(row, NB), :].rearrange("(k p) c -> p k c", p=NP), rows[:, s]).then_inc(rows_out[s], 16)
                    sp.wait_ge(cols_ready, at(r, c + 1))
                    sp.dma_start(T["x_cols"][:, bass.ds(col, 2 * NB)], cols[:, s].rearrange("p a c -> p (a c)")).then_inc(cols_out[s], 16)
                run(sp, NT, 2, store)
                sp.wait_ge(x1_out, 16)
                for o in (rows_out, cols_out):
                    sp.wait_ge(o[0], 16 * ((NT + 1) // 2))
                    sp.wait_ge(o[1], 16 * (NT // 2))

            @block.scalar
            def _(act):
                def grab(r, c):
                    s = c % 2
                    if c >= 2:
                        act.wait_ge(ag_T, at(r, c - 1))
                    nc.scalar.copy(ag[:, s, :], acc[:, bass.ds(at(r, c) * NB, NB)]).then_inc(ag_sb, 1)
                run(act, NT, 2, grab)
                norm_s(act)

                def step(r, c):
                    if r is not None or c < NT:
                        s = c % 2
                        act.wait_ge(h_T, at(r, c + 1))
                        if c >= 2:
                            act.wait_ge(lin_cols, at(r, c - 1))
                        nc.scalar.activation(hT[:, s, :], P[:, 4 + s, 0:NB], ACT.Relu).then_inc(h_T_sb, 1)
                    if r is not None or c >= 1:
                        g, s = c - 1, (c - 1) % 2
                        act.wait_ge(lin_cols, at(r, g + 1))
                        if g >= 2:
                            act.wait_ge(cols_out[s], half(r, g) * 16)
                            act.wait_ge(rows_out[s], half(r, g) * 16)
                        nc.scalar.activation(cols[:, s, 0, :], P[:, 2, 0:NB], ACT.Silu, bias=S["bcol"][:, 0:1])
                        nc.scalar.activation(cols[:, s, 1, :], P[:, 3, 0:NB], ACT.Silu, bias=S["bcol"][:, 1:2]).then_inc(cols_ready, 1)
                        act.wait_ge(pre_ready, at(r, g + 1))
                        nc.scalar.activation(rows[:, s], pre[:, s], ACT.Silu).then_inc(rows_ready, 1)
                run_skewed(act, NT, 1, step)

            @block.vector
            def _(dve):
                def update(r, c):
                    s = c % 2
                    xs = x[:, bass.ds(at(r, c) * NK, NK), :]
                    dve.wait_ge(ag_T, at(r, c + 1))
                    nc.vector.tensor_tensor(xs, xs, P[0:NP, s, :].rearrange("p (k d) -> p k d", k=NK), ALU.add).then_inc(x1_ready, 1)
                    dve.wait_ge(x1_ready, at(r, c + 1))
                    for k in range(NK):
                        t = at(r, c) * NK + k
                        last = nc.vector.bn_stats(stats[:, bass.ds(t, 1), :].rearrange("p t c -> p (t c)"),
                                                  x[:, bass.ds(t, 1), :].rearrange("p t c -> p (t c)"))
                    last.then_inc(st_ready, 1)
                run(dve, NT, 2, update)
                dve.wait_ge(st_ready, NT)
                norm_v(dve)
                nc.vector.memset(acc, 0.0)

                def step(r, c):
                    if r is not None or c < NT:
                        s = c % 2
                        if c >= 2:
                            dve.wait_ge(h_T, at(r, c - 1))
                        for k in range(NK):
                            t = at(r, c) * NK + k
                            last = nc.vector.tensor_scalar(h[:, s, k, :], x[:, bass.ds(t, 1), :].rearrange("p t c -> p (t c)"),
                                                           mean[:, bass.ds(t, 1)], rstd[:, bass.ds(t, 1)], ALU.subtract, ALU.mult)
                        last.then_inc(h_ready, 1)
                    if r is not None or c >= 1:
                        g, s = c - 1, (c - 1) % 2
                        dve.wait_ge(lin_rows, at(r, g + 1))
                        if g >= 2:
                            dve.wait_ge(rows_ready, at(r, g - 1))
                        nc.vector.tensor_tensor(pre[:, s], P[0:NP, 0:2, :].rearrange("p b (k c) -> p (b k) c", k=2),
                                                S["bias_x"][:, :].unsqueeze(1).to_broadcast([NP, NK, 2 * D]), ALU.add).then_inc(pre_ready, 1)
                run_skewed(dve, NT, 1, step)
                dve.wait_ge(x1_out, 16)
                dve.wait_ge(h_ready, NT)
                nc.vector.memset(S["acc"][:, 1, :], 0.0)
                dve.wait_ge(rows_out[0], 16 * ((NT + 1) // 2))
                dve.wait_ge(rows_out[1], 16 * (NT // 2))
                dve.wait_ge(cols_out[0], 16 * ((NT + 1) // 2))
                dve.wait_ge(cols_out[1], 16 * (NT // 2))
                dve.wait_ge(rows_ready, NT)
                nc.vector.memset(S["acc"][:, 2, :], 0.0)

            @block.tensor
            def _(pe):
                def flip(r, c):
                    s = c % 2
                    pe.wait_ge(ag_sb, at(r, c + 1))
                    if c >= 2:
                        pe.wait_ge(x1_ready, at(r, c - 1))
                    for k in range(NK):
                        last = nc.tensor.transpose(P[0:NP, s, k * D:(k + 1) * D], ag[:, s, k * NP:(k + 1) * NP], ident[:, :])
                    last.then_inc(ag_T, 1)
                run(pe, NT, 2, flip)
                pe.wait_ge(x1_ready, NT)

                def step(r, c):
                    if r is not None or c < NT:
                        s = c % 2
                        pe.wait_ge(h_ready, at(r, c + 1))
                        if c >= 2:
                            pe.wait_ge(h_T_sb, at(r, c - 1))
                        for k in range(NK):
                            last = nc.tensor.transpose(P[:, 4 + s, k * NP:(k + 1) * NP], h[:, s, k, :], ident[0:NP, 0:NP])
                        last.then_inc(h_T, 1)
                    if r is not None or c >= 1:
                        g, s = c - 1, (c - 1) % 2
                        pe.wait_ge(h_T_sb, at(r, g + 1))
                        if g >= 1:
                            pe.wait_ge(pre_ready, at(r, g))
                        for k in range(NK):
                            last = nc.tensor.matmul(P[0:NP, k // 2, (k % 2) * 2 * D:(k % 2 + 1) * 2 * D], hT[:, s, k * NP:(k + 1) * NP],
                                                    S["w_x"][:, :], start=True, stop=True)
                        last.then_inc(lin_rows, 1)
                        if g >= 1:
                            pe.wait_ge(cols_ready, at(r, g))
                        for a in range(2):
                            last = nc.tensor.matmul(P[:, 2 + a, 0:NB], S["w_x"][:, a * D:(a + 1) * D], hT[:, s, :], start=True, stop=True)
                        last.then_inc(lin_cols, 1)
                run_skewed(pe, NT, 1, step)


def weighted_edges(nc, T, S, P, N, E):
    G = -(-E // GE)
    with ExitStack() as ctx:
        sem = Sems(nc, ctx, "conv")

        def sb(name, shape, dt=F32):
            return ctx.enter_context(nc.sbuf_tensor(f"conv_{name}", shape, dt))

        acc = S["acc"]
        rows = sb("rows", [128, 4, TPG, 2 * D])
        raw = [sb(f"raw{c}", [128, 2, TPG, FEATS[c]]) for c in range(3)]
        f = sb("f", [128, TPG, FT])
        fT = sb("fT", [FT, 2, TPG, TILE])
        msg = sb("msg", [128, TPG, 3 * D])
        high = sb("high", [128, TPG, 3 * D], F32R)
        low = sb("low", [128, TPG, 3 * D], F32R)
        oh = sb("oh", [128, 2, TPG, WIN], F32R)
        idx = sb("idx", [128, 4, TPG], I32)
        wsum = sb("wsum", [WIN, 3 * D])
        raw_in, rows_in = sem.pair("raw_in"), sem.four("rows_in")
        gathers_begun = sem.one("gathers_begun")
        idx_ready, f_ready, f_T, f_T_sb = sem.one("idx_ready"), sem.one("f_ready"), sem.one("f_T"), sem.one("f_T_sb")
        ew, msg_ready, high_ready, low_ready, sums = (sem.one(x) for x in ("ew", "msg_ready", "high_ready", "low_ready", "sums"))
        oh_ready, added = sem.one("oh_ready"), sem.one("added")
        sums_sb, sums_T = sem.one("sums_sb"), sem.one("sums_T")
        ident = S["ident"]
        FDRAM = (T["edge_attr_24"], T["edge_attr_36"], T["edge_attr_16"])
        start = [sum(FEATS[:c]) for c in range(3)]

        def first_edge(eng, r, c):
            return E - GE if r is None and c == G - 1 else address(eng, r, at(r, c) * GE)

        def live(r, c):
            return r is not None or 0 <= c < G

        with nc.Block() as block:
            @block.sync
            def _(sp):
                def load(r, c):
                    s = c % 2
                    edge = first_edge(sp, r, c)
                    if c >= 2:
                        sp.wait_ge(f_ready, at(r, c - 1))
                    for n in range(3):
                        sp.dma_start(raw[n][:, s], group_rows(FDRAM[n], edge)).then_inc(raw_in[s], 16)
                run(sp, G - 1, 2, load)
                load(None, G - 1)

            @block.gpsimd
            def _(pool):
                def gather(r, c):
                    s = c % 4
                    if c == 0 or c % 2 == G % 2:
                        pool.wait_ge(idx_ready, at(r, 1 if c == 0 and G % 2 else c + 2))
                        if c >= 3:
                            pool.wait_ge(msg_ready, at(r, c - 2) * 2)
                        pool.sem_inc(gathers_begun, 1)
                    for j in range(TPG):
                        nc.gpsimd.indirect_dma_start(rows[:, s, j, :], None, T["x_rows"],
                                                     bass.IndirectOffsetOnAxis(ap=idx[:, c % 4, j:j + 1], axis=0)).then_inc(rows_in[s], 16)
                run(pool, G, 4, gather)

            @block.scalar
            def _(act):
                def indices(r, c):
                    if c >= 4:
                        act.wait_ge(msg_ready, at(r, c - 4) * 2 + 1)
                    nc.scalar.copy(idx[:, c % 4, :], S["src_t"][:, bass.ds(at(r, c), 1), :].rearrange("p g j -> p (g j)")).then_inc(idx_ready, 1)
                indices(None, 0)

                def high_part(r, c, h):
                    g = c - 3
                    act.wait_ge(msg_ready, at(r, g) * 2 + h + 1)
                    if g >= 1:
                        act.wait_ge(sums, at(r, g) * 2 + h - 1)
                    nc.scalar.copy(high[:, 2 * h:2 * h + 2, :], msg[:, 2 * h:2 * h + 2, :]).then_inc(high_ready, 1)

                def step(r, c):
                    if live(r, c - 3):
                        high_part(r, c, 0)
                    if r is not None or c + 1 < G:
                        indices(r, c + 1)
                    if live(r, c - 1):
                        g, s = c - 1, (c - 1) % 2
                        act.wait_ge(f_T, at(r, g + 1))
                        if g >= 2:
                            act.wait_ge(ew, at(r, g - 1) * 2)
                        nc.scalar.copy(fT[:, s], P[0:FT, 4 + s, :].rearrange("p (j e) -> p j e", j=TPG)).then_inc(f_T_sb, 1)
                    if live(r, c - 4):
                        g = c - 4
                        act.wait_ge(sums, at(r, g + 1) * 2)
                        if g >= 1:
                            act.wait_ge(sums_T, at(r, g))
                        nc.scalar.copy(wsum[:, :], P[0:WIN, 6, 0:3 * D]).then_inc(sums_sb, 1)
                    if live(r, c - 3):
                        high_part(r, c, 1)
                    if live(r, c):
                        s = c % 2
                        act.wait_ge(raw_in[s], (half(r, c) + 1) * 48)
                        if c >= 1:
                            act.wait_ge(f_T, at(r, c))
                        for n in range(3):
                            last = nc.scalar.copy(f[:, :, start[n]:start[n] + FEATS[n]], raw[n][:, s])
                        last.then_inc(f_ready, 1)
                run_ahead(act, G, 5, 1, step)

            @block.vector
            def _(dve):
                def products(r, g, h):
                    dve.wait_ge(ew, at(r, g) * 2 + h + 1)
                    if g >= 1:
                        dve.wait_ge(low_ready, at(r, g) * 2 + h - 1)
                    for j in (2 * h, 2 * h + 1):
                        nc.vector.tensor_tensor(msg[:, j, 0:2 * D].rearrange("p (a d) -> p a d", a=2),
                                                P[:, j, 0:2 * D].rearrange("p (a d) -> p a d", a=2),
                                                rows[:, g % 4, j, 0:D].unsqueeze(1).to_broadcast([128, 2, D]), ALU.mult)
                        last = nc.vector.tensor_tensor(msg[:, j, 2 * D:3 * D], P[:, j, 2 * D:3 * D], rows[:, g % 4, j, D:2 * D], ALU.mult)
                    last.then_inc(msg_ready, 1)

                def low_part(r, g, h):
                    part = slice(2 * h, 2 * h + 2)
                    dve.wait_ge(high_ready, at(r, g) * 2 + h + 1)
                    if g >= 1:
                        dve.wait_ge(sums, at(r, g) * 2 + h - 1)
                    nc.vector.tensor_tensor(low[:, part, :], msg[:, part, :], high[:, part, :].bitcast(F32), ALU.subtract).then_inc(low_ready, 1)

                def step(r, c):
                    if live(r, c - 3):
                        g, s = c - 3, (c - 3) % 2
                        if g >= 2:
                            dve.wait_ge(sums, at(r, g - 1) * 2)
                        nc.vector.tensor_tensor(oh[:, s], S["iota"][:, 0:WIN].unsqueeze(1).to_broadcast([128, TPG, WIN]),
                                                S["rel_t"][:, bass.ds(at(r, g), 1), :].rearrange("p g j -> p (g j)").unsqueeze(2).to_broadcast([128, TPG, WIN]),
                                                ALU.is_equal).then_inc(oh_ready, 1)
                        dve.wait_ge(rows_in[g % 4], (quarter(r, g) + 1) * 16 * TPG)
                        products(r, g, 0)
                    if live(r, c - 4):
                        low_part(r, c - 4, 1)
                    if live(r, c - 3):
                        products(r, c - 3, 1)
                    if live(r, c - 5):
                        g = c - 5
                        base = dve.value_load(S["base_i"][0:1, bass.ds(at(r, g), 1)], min_val=0, max_val=N - 1)
                        dve.wait_ge(sums_T, at(r, g + 1))
                        if g >= 1:
                            dve.wait_ge(added, at(r, g))
                        nc.vector.tensor_tensor(acc[:, :, bass.ds(base, WIN)], acc[:, :, bass.ds(base, WIN)],
                                                P[:, 7, 0:3 * WIN].rearrange("p (a w) -> p a w", a=3), ALU.add).then_inc(added, 1)
                    if live(r, c - 3):
                        low_part(r, c - 3, 0)
                run_skewed(dve, G, 5, step)

            @block.tensor
            def _(pe):
                def weights(r, g, h):
                    if h == 0:
                        pe.wait_ge(f_T_sb, at(r, g + 1))
                    if g >= 1:
                        pe.wait_ge(msg_ready, at(r, g) * 2 + h - 1)
                    for j in (2 * h, 2 * h + 1):
                        last = nc.tensor.matmul(P[:, j, 0:3 * D], fT[:, g % 2, j, :], S["w_edge"][:, :], start=True, stop=True)
                    last.then_inc(ew, 1)

                def window_sums(r, g, h):
                    s = g % 2
                    pe.wait_ge(low_ready, at(r, g) * 2 + h + 1)
                    if h == 0:
                        pe.wait_ge(oh_ready, at(r, g + 1))
                        if g >= 1:
                            pe.wait_ge(sums_sb, at(r, g))
                    for j in (2 * h, 2 * h + 1):
                        nc.tensor.matmul(P[0:WIN, 6, 0:3 * D], oh[:, s, j, :], high[:, j, :], start=j == 0, stop=False)
                        last = nc.tensor.matmul(P[0:WIN, 6, 0:3 * D], oh[:, s, j, :], low[:, j, :], start=False, stop=j == TPG - 1)
                    last.then_inc(sums, 1)

                def step(r, c):
                    if live(r, c - 2):
                        weights(r, c - 2, 0)
                    if live(r, c - 1):
                        g, s = c - 1, (c - 1) % 2
                        pe.wait_ge(f_ready, at(r, g + 1))
                        if g >= 2:
                            pe.wait_ge(f_T_sb, at(r, g - 1))
                        for j in range(TPG):
                            last = nc.tensor.transpose(P[0:FT, 4 + s, j * TILE:(j + 1) * TILE], f[:, j, :], ident[:, :])
                        last.then_inc(f_T, 1)
                    if live(r, c - 4):
                        window_sums(r, c - 4, 1)
                    if live(r, c - 2):
                        weights(r, c - 2, 1)
                    if live(r, c - 4):
                        g = c - 4
                        pe.wait_ge(sums_sb, at(r, g + 1))
                        if g >= 1:
                            pe.wait_ge(added, at(r, g))
                    if live(r, c - 3):
                        window_sums(r, c - 3, 0)
                    if live(r, c - 4):
                        for a in range(3):
                            last = nc.tensor.transpose(P[:, 7, a * WIN:(a + 1) * WIN], wsum[:, a * D:(a + 1) * D], ident[0:WIN, 0:WIN])
                        last.then_inc(sums_T, 1)
                run_skewed(pe, G, 5, step)


def node_output(nc, T, S, P, N):
    NT = N // NB
    with ExitStack() as ctx:
        sem = Sems(nc, ctx, "out")

        def sb(name, shape, dt=F32):
            return ctx.enter_context(nc.sbuf_tensor(f"out_{name}", shape, dt))

        acc = S["acc"]
        xc = sb("xc", [D, 2, 2, NB])
        x1 = sb("x1", [NP, 2, NK, D])
        hc = sb("hc", [D, 2, 3, NB])
        o = sb("o", [D, 2, NB])
        w_out = sb("w_out", [D, 7, D])
        w_in = sem.one("w_in")
        xc_in, x1_in, out_done = sem.pair("xc_in"), sem.pair("x1_in"), sem.pair("out_done")
        y, h_act, h_part, h_sum, y3, o_ready, o_T, res = (sem.one(x) for x in ("y", "h_act", "h_part", "h_sum", "y3", "o_ready", "o_T", "res"))
        ident = S["ident"]
        XC = (0, 0, 1)

        def live(r, c):
            return r is not None or 0 <= c < NT

        with nc.Block() as block:
            @block.sync
            def _(sp):
                def load(r, c):
                    if live(r, c):
                        load_cols(r, c)
                    if live(r, c - 2):
                        load_x1(r, c - 2)

                def load_cols(r, c):
                    s = c % 2
                    col = address(sp, r, at(r, c) * 2 * NB)
                    if c >= 2:
                        sp.wait_ge(y, at(r, c - 1) * 3)
                    sp.dma_start(xc[:, s].rearrange("p a c -> p (a c)"), T["x_cols"][:, bass.ds(col, 2 * NB)]).then_inc(xc_in[s], 16)

                def load_x1(r, c):
                    s = c % 2
                    row = address(sp, r, at(r, c) * NB)
                    if c >= 2:
                        sp.wait_ge(out_done[s], half(r, c) * 16)
                    sp.dma_start(x1[:, s], T["x1"][bass.ds(row, NB), :].rearrange("(k p) d -> p k d", p=NP)).then_inc(x1_in[s], 16)
                run_skewed(sp, NT, 2, load)

            @block.gpsimd
            def _(pool):
                def store(r, c):
                    s = c % 2
                    pool.wait_ge(res, at(r, c + 1))
                    pool.dma_start(T["out"][bass.ds(at(r, c) * NB, NB), :].rearrange("(k p) d -> p k d", p=NP), x1[:, s]).then_inc(out_done[s], 16)
                run(pool, NT, 2, store)
                pool.wait_ge(out_done[0], 16 * ((NT + 1) // 2))
                pool.wait_ge(out_done[1], 16 * (NT // 2))

            @block.tensor
            def _(pe):
                pe.wait_ge(w_in, 16)

                def step(r, c):
                    if live(r, c):
                        s = c % 2
                        pe.wait_ge(xc_in[s], (half(r, c) + 1) * 16)
                        for a in range(3):
                            if c >= 1:
                                pe.wait_ge(h_act, at(r, c) * 3 + a - 2)
                            nc.tensor.matmul(P[:, a, 0:NB], w_out[:, a, :], acc[:, a, bass.ds(at(r, c) * NB, NB)], start=True, stop=False)
                            nc.tensor.matmul(P[:, a, 0:NB], w_out[:, 3 + a, :], xc[:, s, XC[a], :], start=False, stop=True).then_inc(y, 1)
                    if live(r, c - 1):
                        g, s = c - 1, (c - 1) % 2
                        pe.wait_ge(h_sum, at(r, g + 1))
                        if g >= 2:
                            pe.wait_ge(o_ready, at(r, g - 1))
                        nc.tensor.matmul(P[:, 3 + s, 0:NB], w_out[:, 6, :], hc[:, s, 0, :], start=True, stop=True).then_inc(y3, 1)
                    if live(r, c - 2):
                        g, s = c - 2, (c - 2) % 2
                        pe.wait_ge(o_ready, at(r, g + 1))
                        if g >= 2:
                            pe.wait_ge(res, at(r, g - 1))
                        for k in range(NK):
                            last = nc.tensor.transpose(P[0:NP, 5 + s, k * D:(k + 1) * D], o[:, s, k * NP:(k + 1) * NP], ident[:, :])
                        last.then_inc(o_T, 1)
                run_skewed(pe, NT, 3, step)

            @block.scalar
            def _(act):
                act.dma_start(w_out[:, :, :].rearrange("p a d -> p (a d)"), T["w_out"]).then_inc(w_in, 16)

                def step(r, c):
                    if live(r, c):
                        s = c % 2
                        if c >= 2:
                            act.wait_ge(y3, at(r, c - 1))
                        for a in range(3):
                            act.wait_ge(y, at(r, c) * 3 + a + 1)
                            nc.scalar.activation(hc[:, s, a, :], P[:, a, 0:NB], ACT.Silu, bias=S["b_h"][:, a:a + 1]).then_inc(h_act, 1)
                    if live(r, c - 1):
                        g, s = c - 1, (c - 1) % 2
                        act.wait_ge(y3, at(r, g + 1))
                        if g >= 2:
                            act.wait_ge(o_T, at(r, g - 1))
                        nc.scalar.activation(o[:, s, :], P[:, 3 + s, 0:NB], ACT.Silu, bias=S["bcol"][:, 2:3]).then_inc(o_ready, 1)
                run_skewed(act, NT, 3, step)

            @block.vector
            def _(dve):
                def step(r, c):
                    if live(r, c - 3):
                        g, s = c - 3, (c - 3) % 2
                        dve.wait_ge(o_T, at(r, g + 1))
                        dve.wait_ge(x1_in[s], (half(r, g) + 1) * 16)
                        nc.vector.tensor_tensor(x1[:, s], P[0:NP, 5 + s, :].rearrange("p (k d) -> p k d", k=NK), x1[:, s], ALU.add).then_inc(res, 1)
                    if live(r, c):
                        s = c % 2
                        dve.wait_ge(h_act, at(r, c) * 3 + 2)
                        nc.vector.tensor_tensor(hc[:, s, 0, :], hc[:, s, 0, :], hc[:, s, 1, :], ALU.add).then_inc(h_part, 1)
                        dve.wait_ge(h_part, at(r, c + 1))
                        dve.wait_ge(h_act, at(r, c) * 3 + 3)
                        nc.vector.tensor_tensor(hc[:, s, 0, :], hc[:, s, 0, :], hc[:, s, 2, :], ALU.add).then_inc(h_sum, 1)
                run_skewed(dve, NT, 3, step)


def gnn_two_layers(nc, T, N, E):
    G = -(-E // GE)
    for name, shape, dt in (("a_rows", [N + WIN, PARTS * 2 * D], BF16), ("b_rows", [N, 2 * D], F32), ("x_rows", [N, 2 * D], F32),
                            ("x_cols", [D, 2 * N], F32), ("x1", [N, D], F32), ("rel_rows", [G, GE], BF16), ("w_out", [D, 7 * D], F32)):
        T[name] = nc.dram_tensor(f"scratch_{name}", shape, dt, kind="Internal").ap()
    with ExitStack() as ctx:
        def sb(name, shape, dt=F32):
            return ctx.enter_context(nc.sbuf_tensor(name, shape, dt))

        P = ctx.enter_context(nc.psum_tensor("P", [128, 8, 512], F32))
        S = {
            "acc": sb("acc", [D, 3, max(N + WIN, N // NP * D)]),
            "rel_t": sb("rel_t", [TILE, G, TPG], BF16), "src_t": sb("src_t", [TILE, G, TPG]),
            "base_i": sb("base_i", [1, G], I32), "base_f": sb("base_f", [128, 4]), "far_i": sb("far_i", [1, 1], I32),
            "ident": sb("ident", [128, 128]), "iota": sb("iota", [128, WIN]), "wrow": sb("wrow", [WROWS, 1]),
            "ones": sb("ones", [128, 1]), "eps": sb("eps", [128, 1]),
            "w_edge": sb("w_edge", [FT, 3 * D]),
            "b_h": sb("b_h", [D, 3]), "bcol": sb("bcol", [D, 3]),
        }
        with ExitStack() as early:
            for name, shape in (("w_ab", [D, 4 * D]), ("w_e", [D, 2 * D]), ("w_x", [D, 2 * D]), ("bias_ab", [NP, 2 * D]), ("bias_x", [NP, 2 * D]), ("w_out", [D, 7 * D])):
                S[name] = early.enter_context(nc.sbuf_tensor(name, shape, F32))
            constants_and_weights(nc, T, S, P, N, E)
            node_tables(nc, T, S, P, N)
            gated_edges(nc, T, S, P, N, E)
            far_edges(nc, T, S, P, N, E, 0)
            node_update(nc, T, S, P, N)
        weighted_edges(nc, T, S, P, N, E)
        far_edges(nc, T, S, P, N, E, 1)
        node_output(nc, T, S, P, N)


def shape_constants(N, E):
    G = -(-E // GE)
    dup = np.zeros((128, GE), np.float32)
    dup[(G - 1) % 128, 0:GE * G - E] = 1.0
    return {
        "c_ident": np.eye(128, dtype=np.float32),
        "c_iota": np.arange(NB, dtype=np.float32),
        "c_wrow": (np.arange(WROWS) // PARTS).astype(np.float32)[:, None],
        "c_dup": dup,
    }


def kernel(**inputs):
    import concourse.bacc as bacc
    from concourse.bass_utils import run_bass_kernel_spmd

    nc = bacc.Bacc("TRN2", target_bir_lowering=False, num_devices=1)
    arrays = {k: np.ascontiguousarray(v) for k, v in inputs.items()}
    N, E = arrays["x"].shape[0], arrays["src"].shape[0]
    arrays.update(shape_constants(N, E))
    T = {k: nc.dram_tensor(f"in_{k}", list(a.shape), mybir.dt.from_np(a.dtype), kind="ExternalInput").ap() for k, a in arrays.items()}
    T["out"] = nc.dram_tensor("out_x", [N, D], F32, kind="ExternalOutput").ap()
    gnn_two_layers(nc, T, N, E)
    r = run_bass_kernel_spmd(nc, [{f"in_{k}": a for k, a in arrays.items()}], core_ids=[0])
    return r.results[0]["out_x"]
```

```python
import numpy as np
import concourse.bass as bass
import concourse.mybir as mybir
from concourse.alu_op_type import AluOpType as ALU
from contextlib import ExitStack

F32, BF16, I32 = mybir.dt.float32, mybir.dt.bfloat16, mybir.dt.int32
F32R = mybir.dt.float32r
ACT = mybir.ActivationFunctionType

D = 128
MID = 64
FEATS = (24, 36, 16)
FT = sum(FEATS)
TILE = 128
TPG = 4
GE = TILE * TPG
WIN = 40
PARTS = 3
WROWS = WIN * PARTS
NP = 125
NK = 4
NB = NP * NK
EPS = 1e-5
EXP_MAX = 80.0
DUP = -1.0e6
UNROLL = 4


def at(r, c):
    return c if r is None else r * UNROLL + c


def half(r, c):
    return c // 2 if r is None else r * (UNROLL // 2) + c // 2


def quarter(r, c):
    return c // UNROLL if r is None else r + c // UNROLL


def run(eng, n, least, step):
    head = min(n, least + (n - least) % UNROLL) if n > least else n
    for c in range(head):
        step(None, c)
    if n > head:
        with eng.Fori(0, (n - head) // UNROLL) as r:
            for u in range(UNROLL):
                step(r, head + u)


def run_skewed(eng, n, skew, step):
    head = skew + 2 + (n - skew - 2) % UNROLL
    for c in range(head):
        step(None, c)
    if n > head:
        with eng.Fori(0, (n - head) // UNROLL) as r:
            for u in range(UNROLL):
                step(r, head + u)
    for c in range(n, n + skew):
        step(None, c)


def address(eng, r, value):
    return value if r is None else eng.snap(value)


def group_rows(x, edge):
    return x[bass.ds(edge, GE), :].rearrange("(p j) d -> p j d", j=TPG)


class Sems:

    def __init__(self, nc, ctx, phase):
        self.nc, self.ctx, self.phase = nc, ctx, phase

    def one(self, name):
        return self.ctx.enter_context(self.nc.semaphore(f"{self.phase}_{name}"))

    def pair(self, name):
        return [self.one(f"{name}{i}") for i in range(2)]

    def four(self, name):
        return [self.one(f"{name}{i}") for i in range(4)]


def constants_and_weights(nc, T, S, P, N, E):
    G = -(-E // GE)
    BLK = 128
    full = G - 1
    nblk = -(-G // BLK)
    rows = [min(BLK, G - BLK * k) for k in range(nblk)]
    with ExitStack() as ctx:
        sem = Sems(nc, ctx, "pre")

        def sb(name, shape, dt=F32):
            return ctx.enter_context(nc.sbuf_tensor(f"pre_{name}", shape, dt))

        IW = 2 * nblk * GE
        idx_i = S["acc"][:, 0, 0:IW].bitcast(I32).rearrange("p (a k c) -> p a k c", a=2, k=nblk)
        idx_f = S["acc"][:, 0, IW:2 * IW].rearrange("p (a k c) -> p a k c", a=2, k=nblk)
        far, far2 = (S["acc"][:, 2, n * nblk * GE:(n + 1) * nblk * GE].rearrange("p (k c) -> p k c", k=nblk) for n in range(2))
        rel16 = sb("rel16", [BLK, nblk, GE], BF16)
        dup = sb("dup", [BLK, GE])
        farsum = sb("farsum", [BLK, 1])
        wf = sb("wf", [D, 3, D])
        ws = sb("ws", [D, 3, D])
        w2 = sb("w2", [D, 2, D])
        wsq = sb("wsq", [D, 3, 3, D])
        w3 = sb("w3", [D, D])
        wa = [sb(f"wa{c}", [MID, FT]) for c in range(3)]
        wb = sb("wb", [D, 3, MID])
        wbT = sb("wbT", [MID, 3, D])
        woT = sb("woT", [D, 3, D])
        bl = sb("bl", [D, 3])
        bo = sb("bo", [D, 3])

        zeroed = sem.one("zeroed")
        idx_in = sem.one("idx_in")
        w_in = sem.one("w_in")
        idx_cast = sem.one("idx_cast")
        idx_rel = sem.one("idx_rel")
        rel_out = sem.one("rel_out")
        tr = sem.one("tr")
        tr_sb = sem.one("tr_sb")
        step_done = sem.one("step_done")
        far_sum = sem.one("far_sum")
        far_tot = sem.one("far_tot")
        wT = sem.one("wT")
        wT_sb = sem.one("wT_sb")
        fold = sem.one("fold")
        fold_sb = sem.one("fold_sb")
        neg = sem.one("neg")

        loads = []
        for part, x in enumerate((T["dst"], T["src"])):
            for k in range(nblk):
                n = min(rows[k], full - BLK * k)
                if n > 0:
                    loads.append((idx_i[0:n, part, k, :], x[BLK * k * GE:(BLK * k + n) * GE].rearrange("(p c) -> p c", c=GE)))
            k, p = full // BLK, full % BLK
            loads.append((idx_i[p:p + 1, part, k, :], x[E - GE:E].rearrange("(p c) -> p c", c=GE)))
        loads.append((S["base_i"][0:1, 0:full], T["dst"][0:full * GE].rearrange("(g c) -> g c", c=GE)[:, 0:1].rearrange("g c -> c g")))
        loads.append((S["base_i"][0:1, full:G], T["dst"][E - GE:E - GE + 1].rearrange("(p c) -> p c", c=1)))
        loads.append((dup[:, :], T["c_dup"]))
        wloads = [
            (S["ident"][:, :], T["c_ident"]), (S["iota"][:, :], T["c_iota"][0:WIN].partition_broadcast(128)),
            (S["wrow"][:, :], T["c_wrow"]),
            (wf[:, :, :], T["L0_gnn_W_f"].rearrange("(k p) n -> p k n", p=D)),
            (ws[:, :, :], T["L0_gnn_W_s"].rearrange("(k p) n -> p k n", p=D)),
            (S["bias_ab"][:, 0:D], T["L0_gnn_b_f"].partition_broadcast(NP)),
            (S["bias_ab"][:, D:2 * D], T["L0_gnn_b_s"].partition_broadcast(NP)),
            (w3[:, :], T["L1_gnn_W_lin3"]),
        ]
        column = lambda x: x.rearrange("(p c) -> p c", c=1)
        for n, x in enumerate(("L1_gnn_b_lin_1", "L1_gnn_b_lin_2", "L1_gnn_b_lin3")):
            wloads.append((S["bcol"][:, n:n + 1], column(T[x])))
        for n, x in enumerate(("L1_gnn_W_lin_1", "L1_gnn_W_lin_2")):
            wloads.append((w2[:, n, :], T[x]))
        start = [sum(FEATS[:c]) for c in range(3)]
        for c in range(3):
            for n, x in enumerate(("Wl", "Wr", "Wo")):
                wloads.append((wsq[:, c, n, :], T[f"L1_gnn_{x}{c}"]))
            wloads.append((wa[c][:, start[c]:start[c] + FEATS[c]], T[f"L1_gnn_Wf{c}a"]))
            wloads.append((wb[:, c, :], T[f"L1_gnn_Wf{c}b"]))
            wloads.append((bl[:, c:c + 1], column(T[f"L1_gnn_bl{c}"])))
            wloads.append((bo[:, c:c + 1], column(T[f"L1_gnn_bo{c}"])))
        NW = 16 * len(wloads)
        NI = 16 * len(loads)
        ident = S["ident"]
        flips = ([(w2[:, n, :], S["w_x"][:, n * D:(n + 1) * D], D) for n in range(2)]
                 + [(w3[:, :], S["w_out"][:, 6 * D:7 * D], D)]
                 + [(wsq[:, c, 2, :], woT[:, c, :], D) for c in range(3)]
                 + [(wb[:, c, :], wbT[:, c, :], MID) for c in range(3)])

        x = S["acc"][0:NP, 1, 0:N // NP * D].rearrange("p (t d) -> p t d", d=D)
        middle = N // NB // 2 * NK
        X_LOADS = ((0, middle), (middle, N // NP))
        x_in = sem.pair("x_in")

        with nc.Block() as block:
            @block.sync
            def _(sp):
                sp.wait_ge(zeroed, 4)
                for o, i in loads:
                    sp.dma_start(o, i, allow_slow_non_contiguous=True).then_inc(idx_in, 16)
                for n, (t0, t1) in enumerate(X_LOADS):
                    sp.dma_start(x[:, t0:t1, :], T["x"][t0 * NP:t1 * NP, :].rearrange("(t p) d -> p t d", p=NP)).then_inc(x_in[n], 16)
                sp.wait_ge(idx_rel, nblk + 3)
                for k in range(nblk):
                    sp.dma_start(T["rel_rows"][BLK * k:BLK * k + rows[k], :], rel16[0:rows[k], k, :]).then_inc(rel_out, 16)
                sp.wait_ge(fold_sb, 12)
                sp.dma_start(T["w_out"], S["w_out"][:, :]).then_inc(rel_out, 16)
                sp.wait_ge(rel_out, 16 * (nblk + 1))

            @block.scalar
            def _(act):
                act.wait_ge(zeroed, 4)
                for o, i in wloads:
                    act.dma_start(o, i, allow_slow_non_contiguous=True).then_inc(w_in, 16)
                for n in range(2 * nblk):
                    part, k = n % 2, n // 2
                    act.wait_ge(tr, n + 1)
                    ps = P[:, n % 4, :].rearrange("p (j g) -> p g j", j=TPG)
                    out = (S["rel_t"], S["src_t"])[part]
                    nc.scalar.copy(out[:, BLK * k:BLK * k + rows[k], :], ps[:, 0:rows[k], :]).then_inc(tr_sb, 1)
                act.wait_ge(far_tot, 1)
                nc.scalar.copy(S["far_i"][0:1, 0:1], P[0:1, 4, 0:1]).then_inc(far_sum, 1)
                for n, (_, o, m) in enumerate(flips):
                    act.wait_ge(wT, n + 1)
                    nc.scalar.copy(o, P[0:m, 5 + n % 2, 0:D]).then_inc(wT_sb, 1)
                for c in range(3):
                    act.wait_ge(fold, c + 1)
                    ps = P[:, c, :]
                    nc.scalar.copy(S["w_edge"][:, c * D:(c + 1) * D], ps[0:FT, 0:D]).then_inc(fold_sb, 1)
                    nc.scalar.copy(S["w_out"][:, c * D:(c + 1) * D], ps[:, D:2 * D]).then_inc(fold_sb, 1)
                    nc.scalar.copy(S["w_out"][:, (3 + c) * D:(4 + c) * D], ps[:, 2 * D:3 * D]).then_inc(fold_sb, 1)
                    nc.scalar.copy(S["b_h"][:, c:c + 1], ps[:, 3 * D:3 * D + 1]).then_inc(fold_sb, 1)

            @block.gpsimd
            def _(pool):
                nc.gpsimd.memset(idx_i[:, :, :, :], 0).then_inc(zeroed, 1)
                for c in range(3):
                    nc.gpsimd.memset(wa[c][:, :], 0.0).then_inc(zeroed, 1)

            @block.vector
            def _(dve):
                nc.vector.memset(S["ones"][:, :], 1.0).then_inc(step_done, 1)
                nc.vector.memset(S["eps"][:, :], EPS)
                dve.wait_ge(idx_in, NI)
                nc.vector.tensor_copy(idx_f[:, :, :, :], idx_i[:, :, :, :]).then_inc(idx_cast, 1)
                dve.wait_ge(idx_cast, 1)
                for k in range(nblk):
                    nc.vector.tensor_copy(S["base_f"][:, k:k + 1], idx_f[:, 0, k, 0:1]).then_inc(idx_cast, 1)
                dve.wait_ge(idx_cast, 1 + nblk)
                for k in range(nblk):
                    nc.vector.tensor_scalar(idx_f[:, 0, k, :], idx_f[:, 0, k, :], S["base_f"][:, k:k + 1], None, ALU.subtract).then_inc(idx_rel, 1)
                dve.wait_ge(idx_rel, nblk)
                nc.vector.tensor_scalar(far[:, :, :], idx_f[:, 0, :, :], float(WIN), None, ALU.is_ge).then_inc(step_done, 1)
                nc.vector.tensor_scalar(far2[:, :, :], idx_f[:, 0, :, :], 0.0, None, ALU.is_lt).then_inc(step_done, 1)
                dve.wait_ge(step_done, 3)
                nc.vector.scalar_tensor_tensor(out=idx_f[:, 0, nblk - 1, :], in0=dup[:, :], scalar=DUP, in1=idx_f[:, 0, nblk - 1, :],
                                               op0=ALU.mult, op1=ALU.add).then_inc(idx_rel, 1)
                nc.vector.tensor_tensor(far[:, :, :], far[:, :, :], far2[:, :, :], ALU.add).then_inc(step_done, 1)
                dve.wait_ge(step_done, 4)
                nc.vector.scalar_tensor_tensor(out=far2[:, 0, :], in0=dup[:, :], scalar=-1.0, in1=far[:, nblk - 1, :],
                                               op0=ALU.mult, op1=ALU.add).then_inc(step_done, 1)
                dve.wait_ge(step_done, 5)
                nc.vector.tensor_scalar(far[:, nblk - 1, :], far2[:, 0, :], 0.0, None, ALU.max).then_inc(step_done, 1)
                dve.wait_ge(idx_rel, nblk + 1)
                nc.vector.tensor_copy(rel16[:, :, :], idx_f[:, 0, :, :]).then_inc(idx_rel, 2)
                dve.wait_ge(step_done, 6)
                nc.vector.tensor_reduce(farsum[:, :], far[:, :, :].rearrange("p k c -> p (k c)"), mybir.AxisListType.X, ALU.add).then_inc(far_sum, 1)
                for n, (t0, t1) in enumerate(X_LOADS):
                    dve.wait_ge(x_in[n], 16)
                    with dve.Fori(0, (t1 - t0) // NK) as i:
                        for k in range(NK):
                            t = i * NK + t0 + k
                            nc.vector.bn_stats(S["stats"][:, bass.ds(t, 1), :].rearrange("p t c -> p (t c)"),
                                               x[:, bass.ds(t, 1), :].rearrange("p t c -> p (t c)"))
                dve.wait_ge(w_in, NW)
                for k, o in ((0, S["w_ab"][:, 0:D]), (1, S["w_ab"][:, 2 * D:3 * D]), (2, S["w_e"][:, 0:D])):
                    nc.vector.tensor_scalar(o, wf[:, k, :], -1.0, None, ALU.mult).then_inc(neg, 1)
                for k, o in ((0, S["w_ab"][:, D:2 * D]), (1, S["w_ab"][:, 3 * D:4 * D]), (2, S["w_e"][:, D:2 * D])):
                    nc.vector.tensor_copy(o, ws[:, k, :]).then_inc(neg, 1)
                nc.vector.tensor_scalar(S["bias_ab"][:, 0:D], S["bias_ab"][:, 0:D], -1.0, None, ALU.mult).then_inc(neg, 1)
                dve.wait_ge(fold_sb, 12)
                nc.vector.tensor_tensor(S["b_h"][:, :], S["b_h"][:, :], bo[:, :], ALU.add)

            @block.tensor
            def _(pe):
                pe.wait_ge(w_in, NW)
                pe.wait_ge(idx_rel, nblk + 1)
                for n in range(2 * nblk):
                    part, k = n % 2, n // 2
                    if n >= 4:
                        pe.wait_ge(tr_sb, n - 3)
                    for j in range(TPG):
                        src = idx_f[0:rows[k], part, k, :].rearrange("g (p j) -> g j p", j=TPG)[:, j, :]
                        last = nc.tensor.transpose(P[:, n % 4, j * BLK:j * BLK + rows[k]], src, ident[0:rows[k], 0:rows[k]])
                    last.then_inc(tr, 1)
                pe.wait_ge(far_sum, 1)
                pe.wait_ge(step_done, 1)
                nc.tensor.matmul(P[0:1, 4, 0:1], farsum[:, 0:1], S["ones"][:, 0:1], start=True, stop=True).then_inc(far_tot, 1)
                for n, (i, _, m) in enumerate(flips):
                    if n >= 2:
                        pe.wait_ge(wT_sb, n - 1)
                    nc.tensor.transpose(P[0:m, 5 + n % 2, 0:D], i, ident[:, :]).then_inc(wT, 1)
                pe.wait_ge(wT_sb, len(flips))
                pe.wait_ge(tr_sb, 2 * nblk)
                for c in range(3):
                    ps = P[:, c, :]
                    nc.tensor.matmul(ps[0:FT, 0:D], wa[c][:, :], wbT[:, c, :], start=True, stop=True)
                    nc.tensor.matmul(ps[:, D:2 * D], wsq[:, c, 0, :], woT[:, c, :], start=True, stop=True)
                    nc.tensor.matmul(ps[:, 2 * D:3 * D], wsq[:, c, 1, :], woT[:, c, :], start=True, stop=True)
                    nc.tensor.matmul(ps[:, 3 * D:3 * D + 1], woT[:, c, :], bl[:, c:c + 1], start=True, stop=True).then_inc(fold, 1)


def norm_scales(nc, sem, stats, mean, rstd, tmp, eps, nt):
    chain = sem.one("ln_chain")
    var_ready = sem.one("ln_var")
    sqrt_ready = sem.one("ln_sqrt")
    m0, v0, m1, v1 = (stats[:, :, i:i + 1].rearrange("p t c -> p (t c)") for i in (1, 2, 4, 5))

    def vector(dve):
        def link(i, n):
            i.then_inc(chain, 1)
            dve.wait_ge(chain, n)
        link(nc.vector.tensor_tensor(mean[:, :], m0, m1, ALU.add), 1)
        link(nc.vector.tensor_tensor(tmp[:, 0, :], m0, m1, ALU.subtract), 2)
        link(nc.vector.tensor_scalar(mean[:, :], mean[:, :], 0.5, None, ALU.mult), 3)
        link(nc.vector.scalar_tensor_tensor(out=tmp[:, 0, :], in0=tmp[:, 0, :], scalar=0.25, in1=tmp[:, 0, :], op0=ALU.mult, op1=ALU.mult), 4)
        link(nc.vector.tensor_tensor(tmp[:, 1, :], v0, v1, ALU.add), 5)
        nc.vector.scalar_tensor_tensor(out=tmp[:, 0, :], in0=tmp[:, 1, :], scalar=1.0 / D, in1=tmp[:, 0, :], op0=ALU.mult, op1=ALU.add).then_inc(var_ready, 1)
        dve.wait_ge(sqrt_ready, 1)
        nc.vector.reciprocal(rstd[:, :], tmp[:, 1, :]).then_inc(chain, 1)
        dve.wait_ge(chain, 6)

    def scalar(act):
        act.wait_ge(var_ready, 1)
        nc.scalar.activation(tmp[:, 1, :], tmp[:, 0, :], ACT.Sqrt, bias=eps[0:NP, 0:1], scale=1.0).then_inc(sqrt_ready, 1)

    return vector, scalar


def node_tables(nc, T, S, P, N):
    NT = N // NB
    with ExitStack() as ctx:
        sem = Sems(nc, ctx, "nodes")

        def sb(name, shape, dt=F32):
            return ctx.enter_context(nc.sbuf_tensor(f"nodes_{name}", shape, dt))

        x = S["acc"][0:NP, 1, 0:NT * NK * D].rearrange("p (t d) -> p t d", d=D)
        stats = S["stats"]
        mean, rstd = sb("mean", [NP, NT * NK]), sb("rstd", [NP, NT * NK])
        tmp = sb("tmp", [NP, 2, NT * NK])
        room = S["acc"][0:NP, 2, :]
        a_f = room[:, 0:4096].rearrange("p (s k c) -> p s k c", s=4, k=NK)
        b_st = room[:, 4096:6144].rearrange("p (s k c) -> p s k c", s=2, k=NK)
        h = room[:, 6144:7168].rearrange("p (s k c) -> p s k c", s=2, k=NK)
        hT = S["acc"][:, 2, 7168:7168 + 2 * NB].rearrange("p (s c) -> p s c", s=2)
        a_st = sb("a_st", [NP, 4, NK, PARTS, 2 * D], BF16)
        pad = sb("pad", [WIN, PARTS * 2 * D], BF16)
        h_ready, xh_ready = sem.one("h_ready"), sem.one("xh_ready")
        h_T, h_T_sb = sem.one("h_T"), sem.one("h_T_sb")
        ab, b_ready, af_ready = sem.one("ab"), sem.one("b_ready"), sem.one("af_ready")
        hi, mid_res, mid, lo = sem.one("hi"), sem.one("mid_res"), sem.one("mid"), sem.one("lo")
        a_out, b_out = sem.four("a_out"), sem.pair("b_out")
        zero, pad_out = sem.one("zero"), sem.one("pad_out")
        norm_v, norm_s = norm_scales(nc, sem, stats, mean, rstd, tmp, S["eps"], NT * NK)
        ident = S["ident"]

        def live(r, c):
            return r is not None or 0 <= c < NT

        with nc.Block() as block:
            @block.sync
            def _(sp):
                sp.wait_ge(zero, 1)
                sp.dma_start(T["a_rows"][N:N + WIN, :], pad[:, :]).then_inc(pad_out, 16)

                def store(r, c):
                    if live(r, c):
                        s = c % 2
                        row = address(sp, r, at(r, c) * NB)
                        sp.wait_ge(b_ready, at(r, c + 1) * 2)
                        sp.dma_start(T["b_rows"][bass.ds(row, NB), :].rearrange("(k p) c -> p k c", p=NP), b_st[:, s]).then_inc(b_out[s], 16)
                    if live(r, c - 2):
                        g, s = c - 2, (c - 2) % 4
                        row = address(sp, r, at(r, g) * NB)
                        sp.wait_ge(lo, at(r, g + 1))
                        sp.dma_start(T["a_rows"][bass.ds(row, NB), :].rearrange("(k p) c -> p k c", p=NP),
                                     a_st[:, s].rearrange("p k a c -> p k (a c)")).then_inc(a_out[s], 16)
                run_skewed(sp, NT, 3, store)
                sp.wait_ge(pad_out, 16)
                for n in range(4):
                    sp.wait_ge(a_out[n], 16 * ((NT + 3 - n) // 4))
                for n in range(2):
                    sp.wait_ge(b_out[n], 16 * ((NT + 1 - n) // 2))

            @block.vector
            def _(dve):
                norm_v(dve)

                def front(r, c):
                    s = c % 2
                    if c >= 2:
                        dve.wait_ge(h_T, at(r, c - 1))
                        dve.wait_ge(xh_ready, at(r, c - 1))
                    for k in range(NK):
                        t = at(r, c) * NK + k
                        last = nc.vector.tensor_scalar(h[:, s, k, :], x[:, bass.ds(t, 1), :].rearrange("p t c -> p (t c)"),
                                                       mean[:, bass.ds(t, 1)], rstd[:, bass.ds(t, 1)], ALU.subtract, ALU.mult)
                    last.then_inc(h_ready, 1)

                def xh(r, c):
                    xs = x[:, bass.ds(at(r, c) * NK, NK), :]
                    dve.wait_ge(h_ready, at(r, c + 1))
                    nc.vector.scalar_tensor_tensor(out=xs, in0=h[:, c % 2], scalar=0.0, in1=xs, op0=ALU.max, op1=ALU.add).then_inc(xh_ready, 1)

                def table(r, c):
                    if c >= 4:
                        dve.wait_ge(lo, at(r, c - 3))
                    for b in range(2):
                        dve.wait_ge(ab, at(r, c) * 2 + b + 1)
                        nc.vector.tensor_tensor(a_f[:, c % 4, 2 * b:2 * b + 2], P[0:NP, b, :].rearrange("p (k c) -> p k c", k=2),
                                                S["bias_ab"][:, :].unsqueeze(1).to_broadcast([NP, 2, 2 * D]), ALU.add).then_inc(af_ready, 1)

                def third_part(r, c):
                    s = c % 4
                    dve.wait_ge(mid, at(r, c + 1))
                    nc.vector.tensor_tensor(a_st[:, s, :, 2, :], a_f[:, s], a_st[:, s, :, 1, :], ALU.subtract).then_inc(lo, 1)

                def step(r, c):
                    if live(r, c):
                        front(r, c)
                        xh(r, c)
                    if live(r, c - 4):
                        third_part(r, c - 4)
                    if live(r, c - 2):
                        table(r, c - 2)
                run_skewed(dve, NT, 4, step)

            @block.scalar
            def _(act):
                norm_s(act)

                def step(r, c):
                    if live(r, c - 2):
                        g, s = c - 2, (c - 2) % 2
                        if g >= 2:
                            act.wait_ge(b_out[s], half(r, g) * 16)
                        for b in range(2):
                            act.wait_ge(ab, at(r, g) * 2 + b + 1)
                            nc.scalar.copy(b_st[:, s, 2 * b:2 * b + 2], P[0:NP, 2 + b, :].rearrange("p (k c) -> p k c", k=2)).then_inc(b_ready, 1)
                    if live(r, c):
                        s = c % 2
                        act.wait_ge(h_T, at(r, c + 1))
                        if c >= 2:
                            act.wait_ge(ab, at(r, c - 1) * 2)
                        nc.scalar.activation(hT[:, s, :], P[:, 4 + s, 0:NB], ACT.Relu).then_inc(h_T_sb, 1)
                    if live(r, c - 3):
                        g, s = c - 3, (c - 3) % 4
                        act.wait_ge(mid_res, at(r, g + 1))
                        nc.scalar.copy(a_st[:, s, :, 1, :], a_f[:, s]).then_inc(mid, 1)
                    if live(r, c - 2):
                        g, s = c - 2, (c - 2) % 4
                        act.wait_ge(af_ready, at(r, g + 1) * 2)
                        if g >= 4:
                            act.wait_ge(a_out[s], quarter(r, g) * 16)
                        nc.scalar.copy(a_st[:, s, :, 0, :], a_f[:, s]).then_inc(hi, 1)
                run_skewed(act, NT, 4, step)

            @block.gpsimd
            def _(pool):
                nc.gpsimd.memset(pad[:, :], 0.0).then_inc(zero, 1)
                nc.gpsimd.memset(S["acc"][:, 0, :], 0.0)

                def second_part(r, c):
                    s = c % 4
                    pool.wait_ge(hi, at(r, c + 1))
                    nc.gpsimd.tensor_tensor(a_f[:, s], a_f[:, s], a_st[:, s, :, 0, :], ALU.subtract).then_inc(mid_res, 1)
                run(pool, NT, 4, second_part)

            @block.tensor
            def _(pe):
                def step(r, c):
                    if live(r, c - 2):
                        g, s = c - 2, (c - 2) % 2
                        pe.wait_ge(h_T_sb, at(r, g + 1))
                        for b in range(2):
                            if g >= 1:
                                pe.wait_ge(b_ready, at(r, g) * 2 + b - 1)
                                pe.wait_ge(af_ready, at(r, g) * 2 + b - 1)
                            for k in (2 * b, 2 * b + 1):
                                for a in range(2):
                                    bank = P[0:NP, 2 * a + b, (k % 2) * 2 * D:(k % 2 + 1) * 2 * D]
                                    last = nc.tensor.matmul(bank, hT[:, s, k * NP:(k + 1) * NP], S["w_ab"][:, 2 * a * D:2 * (a + 1) * D], start=True, stop=True)
                            last.then_inc(ab, 1)
                    if live(r, c):
                        s = c % 2
                        pe.wait_ge(h_ready, at(r, c + 1))
                        if c >= 2:
                            pe.wait_ge(h_T_sb, at(r, c - 1))
                        for k in range(NK):
                            last = nc.tensor.transpose(P[:, 4 + s, k * NP:(k + 1) * NP], h[:, s, k, :], ident[0:NP, 0:NP])
                        last.then_inc(h_T, 1)
                run_skewed(pe, NT, 4, step)


def gated_edges(nc, T, S, P, N, E):
    G = -(-E // GE)
    with ExitStack() as ctx:
        sem = Sems(nc, ctx, "gate")

        def sb(name, shape, dt=F32):
            return ctx.enter_context(nc.sbuf_tensor(f"gate_{name}", shape, dt))

        acc = S["acc"][:, 0, :]
        room = S["acc"][:, 2, :]
        z = room[:, 0:2048].rearrange("p (s j c) -> p s j c", s=2, j=TPG)
        e = room[:, 2048:4096].rearrange("p (s j c) -> p s j c", s=2, j=TPG)
        rows = room[:, 4096:8192].rearrange("p (s j c) -> p s j c", s=4, j=TPG)
        msg = room[:, 8192:9216].rearrange("p (s j c) -> p s j c", s=2, j=TPG)
        ea = sb("ea", [128, 2, TPG, D])
        eaT = sb("eaT", [128, 2, TPG, TILE])
        win = sb("win", [WROWS, 2, 2 * D], BF16)
        relb = sb("relb", [WROWS, 2, GE], BF16)
        ohT = sb("ohT", [WROWS, 2, GE], BF16)
        oh = sb("oh", [128, 2, TPG, WIN])
        idx = sb("idx", [128, 4, TPG], I32)
        wsum = sb("wsum", [WIN, D])
        ea_in, win_in, relb_in = (sem.pair(x) for x in ("ea_in", "win_in", "relb_in"))
        rows_in = sem.four("rows_in")
        gathers_begun = sem.one("gathers_begun")
        idx_ready, ea_T, ea_T_sb = sem.one("idx_ready"), sem.one("ea_T"), sem.one("ea_T_sb")
        ohT_ready, oh_ready, z_psum, z_sum = sem.one("ohT_ready"), sem.one("oh_ready"), sem.one("z_psum"), sem.one("z_sum")
        clamped, exp_done, ln_done, gate = sem.one("clamped"), sem.one("exp_done"), sem.one("ln_done"), sem.one("gate")
        val, msg_ready, added = sem.one("val"), sem.one("msg_ready"), sem.one("added")
        sums, sums_sb, sums_T = sem.one("sums"), sem.one("sums_sb"), sem.one("sums_T")
        ident = S["ident"]

        def first_edge(eng, r, c):
            return E - GE if r is None and c == G - 1 else address(eng, r, at(r, c) * GE)

        def live(r, c):
            return r is not None or 0 <= c < G

        with nc.Block() as block:
            @block.sync
            def _(sp):
                def load(r, c):
                    s = c % 2
                    edge = first_edge(sp, r, c)
                    group = address(sp, r, at(r, c))
                    rel_row = address(sp, r, at(r, c) * GE)
                    base = sp.value_load(S["base_i"][0:1, bass.ds(group, 1)], min_val=0, max_val=N - 1)
                    window = address(sp, 0, base * PARTS)
                    if c >= 2:
                        sp.wait_ge(ea_T, at(r, c - 1))
                    sp.dma_start(ea[:, s], group_rows(T["edge_attr_128"], edge)).then_inc(ea_in[s], 16)
                    if c >= 2:
                        sp.wait_ge(ohT_ready, at(r, c - 1))
                        sp.wait_ge(z_psum, at(r, c - 1))
                    sp.dma_start(win[:, s, :], T["a_rows"].rearrange("n (a c) -> (n a) c", a=PARTS)[bass.ds(window, WROWS), :]).then_inc(win_in[s], 16)
                    sp.dma_start(relb[:, s, :], T["rel_rows"].rearrange("g c -> (g c)")[bass.ds(rel_row, GE)].partition_broadcast(WROWS)).then_inc(relb_in[s], 16)
                run(sp, G - 1, 2, load)
                load(None, G - 1)

            @block.gpsimd
            def _(pool):
                def gather(r, c):
                    s = c % 4
                    if c == 0 or c % 2 == G % 2:
                        pool.wait_ge(idx_ready, at(r, 1 if c == 0 and G % 2 else c + 2))
                        if c >= 3:
                            pool.wait_ge(z_sum, at(r, c - 2))
                        pool.sem_inc(gathers_begun, 1)
                    for j in range(TPG):
                        nc.gpsimd.indirect_dma_start(rows[:, s, j, :], None, T["b_rows"],
                                                     bass.IndirectOffsetOnAxis(ap=idx[:, c % 4, j:j + 1], axis=0)).then_inc(rows_in[s], 16)
                run(pool, G, 4, gather)

            @block.scalar
            def _(act):
                nc.scalar.preload_act_table_set("natural_log_exp_and_others")

                def indices(r, c):
                    if c >= 4:
                        act.wait_ge(z_sum, at(r, c - 3))
                    nc.scalar.copy(idx[:, c % 4, :], S["src_t"][:, bass.ds(at(r, c), 1), :].rearrange("p g j -> p (g j)")).then_inc(idx_ready, 1)
                indices(None, 0)
                indices(None, 1)

                def step(r, c):
                    if (r is None and c + 2 < G) or (r is not None):
                        indices(r, c + 2)
                    if live(r, c):
                        s = c % 2
                        act.wait_ge(ea_T, at(r, c + 1))
                        if c >= 2:
                            act.wait_ge(z_psum, at(r, c - 1))
                        nc.scalar.copy(eaT[:, s], P[:, 4 + s, :].rearrange("p (j e) -> p j e", j=TPG)).then_inc(ea_T_sb, 1)
                    if live(r, c - 1):
                        s = (c - 1) % 2
                        act.wait_ge(clamped, at(r, c))
                        nc.scalar.activation(e[:, s], e[:, s], ACT.Exp).then_inc(exp_done, 1)
                    if live(r, c - 3):
                        g = c - 3
                        act.wait_ge(sums, at(r, g + 1))
                        if g >= 1:
                            act.wait_ge(sums_T, at(r, g))
                        nc.scalar.copy(wsum[:, :], P[0:WIN, 6, 0:D]).then_inc(sums_sb, 1)
                    if live(r, c - 1):
                        s = (c - 1) % 2
                        act.wait_ge(exp_done, at(r, c))
                        nc.scalar.activation(e[:, s], e[:, s], ACT.Ln, bias=1.0).then_inc(ln_done, 1)
                        act.wait_ge(ln_done, at(r, c))
                        nc.scalar.activation(e[:, s, :, 0:D], e[:, s, :, 0:D], ACT.Exp, scale=-1.0).then_inc(gate, 1)
                run_ahead(act, G, 5, 2, step)

            @block.vector
            def _(dve):
                def step(r, c):
                    if live(r, c):
                        s = c % 2
                        dve.wait_ge(relb_in[s], (half(r, c) + 1) * 16)
                        if c >= 2:
                            dve.wait_ge(z_psum, at(r, c - 1))
                        nc.vector.tensor_scalar(ohT[:, s, :], relb[:, s, :], S["wrow"][:, 0:1], None, ALU.is_equal).then_inc(ohT_ready, 1)
                    if live(r, c - 1):
                        g, s = c - 1, (c - 1) % 2
                        dve.wait_ge(z_psum, at(r, g + 1))
                        dve.wait_ge(rows_in[g % 4], (quarter(r, g) + 1) * 16 * TPG)
                        if g >= 2:
                            dve.wait_ge(val, at(r, g - 1))
                        nc.vector.tensor_tensor(z[:, s], P[:, 2 * s:2 * s + 2, :].rearrange("p b (j c) -> p (b j) c", j=2), rows[:, g % 4], ALU.add).then_inc(z_sum, 1)
                        dve.wait_ge(z_sum, at(r, g + 1))
                        if g >= 2:
                            dve.wait_ge(msg_ready, at(r, g - 1))
                        nc.vector.tensor_scalar(e[:, s], z[:, s], EXP_MAX, None, ALU.min).then_inc(clamped, 1)
                    if live(r, c - 2):
                        g, s = c - 2, c % 2
                        if g >= 2:
                            dve.wait_ge(sums, at(r, g - 1))
                        nc.vector.tensor_tensor(oh[:, s], S["iota"][:, 0:WIN].unsqueeze(1).to_broadcast([128, TPG, WIN]),
                                                S["rel_t"][:, bass.ds(at(r, g), 1), :].rearrange("p g j -> p (g j)").unsqueeze(2).to_broadcast([128, TPG, WIN]),
                                                ALU.is_equal).then_inc(oh_ready, 1)
                    if live(r, c - 4):
                        g = c - 4
                        base = dve.value_load(S["base_i"][0:1, bass.ds(at(r, g), 1)], min_val=0, max_val=N - 1)
                        dve.wait_ge(sums_T, at(r, g + 1))
                        if g >= 1:
                            dve.wait_ge(added, at(r, g))
                        nc.vector.tensor_tensor(acc[:, bass.ds(base, WIN)], acc[:, bass.ds(base, WIN)], P[:, 7, 0:WIN], ALU.add).then_inc(added, 1)
                    if live(r, c - 2):
                        g, s = c - 2, c % 2
                        dve.wait_ge(ln_done, at(r, g + 1))
                        nc.vector.tensor_tensor(e[:, s, :, D:2 * D], e[:, s, :, D:2 * D], z[:, s, :, D:2 * D], ALU.max).then_inc(val, 1)
                        dve.wait_ge(val, at(r, g + 1))
                        dve.wait_ge(gate, at(r, g + 1))
                        nc.vector.tensor_tensor(msg[:, s], e[:, s, :, 0:D], e[:, s, :, D:2 * D], ALU.mult).then_inc(msg_ready, 1)
                run_skewed(dve, G, 5, step)

            @block.tensor
            def _(pe):
                def step(r, c):
                    if live(r, c):
                        s = c % 2
                        pe.wait_ge(ea_in[s], (half(r, c) + 1) * 16)
                        if c >= 2:
                            pe.wait_ge(ea_T_sb, at(r, c - 1))
                        for j in range(TPG):
                            last = nc.tensor.transpose(P[:, 4 + s, j * TILE:(j + 1) * TILE], ea[:, s, j, :], ident[:, :])
                        last.then_inc(ea_T, 1)
                    if live(r, c - 1):
                        g, s = c - 1, (c - 1) % 2
                        pe.wait_ge(ea_T_sb, at(r, g + 1))
                        pe.wait_ge(win_in[s], (half(r, g) + 1) * 16)
                        pe.wait_ge(ohT_ready, at(r, g + 1))
                        if g >= 2:
                            pe.wait_ge(z_sum, at(r, g - 1))
                        tile_oh = ohT[:, s, :].rearrange("w (p j) -> w j p", j=TPG)
                        for j in range(TPG):
                            zp = P[:, 2 * s + j // 2, (j % 2) * 2 * D:(j % 2 + 1) * 2 * D]
                            nc.tensor.matmul(zp, eaT[:, s, j, :], S["w_e"][:, :], start=True, stop=False)
                            last = nc.tensor.matmul(zp, tile_oh[:, j, :], win[:, s, :], start=False, stop=True)
                        last.then_inc(z_psum, 1)
                    if live(r, c - 4):
                        g = c - 4
                        pe.wait_ge(sums_sb, at(r, g + 1))
                        if g >= 1:
                            pe.wait_ge(added, at(r, g))
                    if live(r, c - 3):
                        g, s = c - 3, (c - 3) % 2
                        pe.wait_ge(msg_ready, at(r, g + 1))
                        pe.wait_ge(oh_ready, at(r, g + 1))
                        if g >= 1:
                            pe.wait_ge(sums_sb, at(r, g))
                        for j in range(TPG):
                            last = nc.tensor.matmul(P[0:WIN, 6, 0:D], oh[:, s, j, :], msg[:, s, j, :], start=j == 0, stop=j == TPG - 1)
                        last.then_inc(sums, 1)
                    if live(r, c - 4):
                        nc.tensor.transpose(P[:, 7, 0:WIN], wsum[:, :], ident[0:WIN, 0:WIN]).then_inc(sums_T, 1)
                run_skewed(pe, G, 5, step)


def run_ahead(eng, n, skew, ahead, step):
    head = skew + 2 + (n - ahead - skew - 2) % UNROLL
    for c in range(head):
        step(None, c)
    if n - ahead > head:
        with eng.Fori(0, (n - ahead - head) // UNROLL) as r:
            for u in range(UNROLL):
                step(r, head + u)
    for c in range(n - ahead, n + skew):
        step(None, c)


def far_edges(nc, T, S, P, N, E, layer):
    G, NT = -(-E // GE), N // NB
    FAR = 1.0e6
    accs = 1 if layer == 0 else 3
    with ExitStack() as ctx:
        sem = Sems(nc, ctx, f"far{layer}")
        room = [0]

        def sb(name, shape, dt=F32):
            if layer == 1:
                return ctx.enter_context(nc.sbuf_tensor(f"far_{name}", [128] + shape, dt))[:]
            n = int(np.prod(shape)) // (2 if dt == BF16 else 1)
            flat = S["acc"][:, 2, room[0]:room[0] + n]
            room[0] += n
            names = "abc"[:len(shape)]
            flat = flat if dt == F32 else flat.bitcast(dt)
            return flat.rearrange(f"p ({' '.join(names)}) -> p {' '.join(names)}", **dict(zip(names, shape)))

        rows = sb("rows", [TPG, 2 * D])
        msg = sb("msg", [TPG, accs * D])
        oh = sb("oh", [TPG, NB])
        iota = sb("iota", [NB])
        dst_i, src_i = sb("dst_i", [TPG], I32), sb("src_i", [TPG], I32)
        dst_f, near, mark = sb("dst_f", [TPG]), sb("near", [TPG]), sb("mark", [TPG])
        if layer == 0:
            z, e = sb("z", [TPG, 2 * D]), sb("e", [TPG, 2 * D])
            parts = sb("parts", [TPG, PARTS * 2 * D], BF16)
            ea, eaT = sb("ea", [TPG, D]), sb("eaT", [TPG, TILE])
            streams = ((ea, T["edge_attr_128"]),)
        else:
            raw = [sb(f"raw{c}", [TPG, FEATS[c]]) for c in range(3)]
            f, fT = sb("f", [TPG, FT]), sb("fT", [TPG, TILE])
            streams = tuple(zip(raw, (T["edge_attr_24"], T["edge_attr_36"], T["edge_attr_16"])))
        start = [sum(FEATS[:c]) for c in range(3)]
        LOADS = len(streams) + 2
        GATHERS = TPG * (2 if layer == 0 else 1)
        iota_in, free, loaded, begun, gathered = (sem.one(x) for x in ("iota_in", "free", "loaded", "begun", "gathered"))
        repacked, flipped, flipped_sb, product = (sem.one(x) for x in ("repacked", "flipped", "flipped_sb", "product"))
        clamped, act_chain, chain, oh_ready, shifted, sums, added = (sem.one(x) for x in ("clamped", "act_chain", "chain", "oh_ready", "shifted", "sums", "added"))
        ident = S["ident"]

        def if_any(eng, body):
            left = eng.value_load(S["far_i"][0:1, 0:1], min_val=0, max_val=E)
            with eng.If(left > 0):
                if G > 1:
                    with eng.Fori(0, G - 1) as g:
                        body(g, g * GE)
                body(G - 1, E - GE)

        with nc.Block() as block:
            @block.sync
            def _(sp):
                sp.dma_start(iota, T["c_iota"].partition_broadcast(128)).then_inc(iota_in, 16)
                sp.wait_ge(iota_in, 16)

                def load(g, edge):
                    edge = edge if type(edge) is int else sp.snap(edge)
                    row = edge if type(edge) is int else sp.snap(edge)
                    sp.wait_ge(free, g + 1)
                    for to, of in streams:
                        sp.dma_start(to, group_rows(of, edge)).then_inc(loaded, 16)
                    for to, of in ((dst_i, T["dst"]), (src_i, T["src"])):
                        sp.dma_start(to, of[bass.ds(row, GE)].rearrange("(p j) -> p j", j=TPG)).then_inc(loaded, 16)
                if_any(sp, load)

            @block.gpsimd
            def _(pool):
                def gather(g, edge):
                    pool.wait_ge(loaded, g * 16 * LOADS + 16 * LOADS)
                    pool.sem_inc(begun, 1)
                    for j in range(TPG):
                        by_src = bass.IndirectOffsetOnAxis(ap=src_i[:, j:j + 1], axis=0)
                        by_dst = bass.IndirectOffsetOnAxis(ap=dst_i[:, j:j + 1], axis=0)
                        nc.gpsimd.indirect_dma_start(rows[:, j, :], None, T["b_rows" if layer == 0 else "x_rows"], by_src).then_inc(gathered, 16)
                        if layer == 0:
                            nc.gpsimd.indirect_dma_start(parts[:, j, :], None, T["a_rows"], by_dst).then_inc(gathered, 16)
                if_any(pool, gather)

            @block.scalar
            def _(act):
                def messages(g, edge):
                    if layer == 0:
                        act.wait_ge(flipped, g + 1)
                        nc.scalar.copy(eaT, P[:, 4, :].rearrange("p (j e) -> p j e", j=TPG)).then_inc(flipped_sb, 1)
                        act.wait_ge(clamped, g + 1)
                        nc.scalar.activation(e, e, ACT.Exp).then_inc(act_chain, 1)
                        act.wait_ge(act_chain, g * 3 + 1)
                        nc.scalar.activation(e, e, ACT.Ln, bias=1.0).then_inc(act_chain, 1)
                        act.wait_ge(act_chain, g * 3 + 2)
                        nc.scalar.activation(e[:, :, 0:D], e[:, :, 0:D], ACT.Exp, scale=-1.0).then_inc(act_chain, 1)
                    else:
                        act.wait_ge(loaded, g * 16 * LOADS + 16 * LOADS)
                        for n in range(3):
                            last = nc.scalar.copy(f[:, :, start[n]:start[n] + FEATS[n]], raw[n])
                        last.then_inc(repacked, 1)
                        act.wait_ge(flipped, g + 1)
                        nc.scalar.copy(fT[0:FT], P[0:FT, 4, :].rearrange("p (j e) -> p j e", j=TPG)).then_inc(flipped_sb, 1)
                if_any(act, messages)

            @block.tensor
            def _(pe):
                def products(g, edge):
                    if layer == 0:
                        pe.wait_ge(loaded, g * 16 * LOADS + 16 * LOADS)
                        for j in range(TPG):
                            last = nc.tensor.transpose(P[:, 4, j * TILE:(j + 1) * TILE], ea[:, j, :], ident[:, :])
                        last.then_inc(flipped, 1)
                        pe.wait_ge(flipped_sb, g + 1)
                        for j in range(TPG):
                            last = nc.tensor.matmul(P[:, j // 2, (j % 2) * 2 * D:(j % 2 + 1) * 2 * D], eaT[:, j, :], S["w_e"][:, :], start=True, stop=True)
                        last.then_inc(product, 1)
                    else:
                        pe.wait_ge(repacked, g + 1)
                        for j in range(TPG):
                            last = nc.tensor.transpose(P[0:FT, 4, j * TILE:(j + 1) * TILE], f[:, j, :], ident[:, :])
                        last.then_inc(flipped, 1)
                        pe.wait_ge(flipped_sb, g + 1)
                        for j in range(TPG):
                            last = nc.tensor.matmul(P[:, j, 0:3 * D], fT[0:FT, j, :], S["w_edge"][:, :], start=True, stop=True)
                        last.then_inc(product, 1)
                    with pe.Fori(0, NT) as b:
                        pe.wait_ge(oh_ready, g * NT + b + 1)
                        for a in range(accs):
                            for j in range(TPG):
                                last = nc.tensor.matmul(P[:, 5 + a, 0:NB], msg[:, j, a * D:(a + 1) * D], oh[:, j, :], start=j == 0, stop=j == TPG - 1)
                        last.then_inc(sums, 1)
                if_any(pe, products)

            @block.vector
            def _(dve):
                dve.wait_ge(iota_in, 16)
                dve.sem_inc(free, 1)

                def spread(g, edge):
                    done = [0]
                    LINKS = 11 if layer == 0 else 6

                    def link(i):
                        done[0] += 1
                        i.then_inc(chain, 1)
                        dve.wait_ge(chain, g * LINKS + done[0])
                    dve.wait_ge(loaded, g * 16 * LOADS + 16 * LOADS)
                    rel = S["rel_t"][:, bass.ds(g, 1), :].rearrange("p g j -> p (g j)")
                    link(nc.vector.tensor_scalar(near, rel, 0.0, None, ALU.is_ge))
                    link(nc.vector.tensor_scalar(mark, rel, float(WIN), None, ALU.is_lt))
                    link(nc.vector.tensor_tensor(near, near, mark, ALU.mult))
                    link(nc.vector.scalar_tensor_tensor(out=near, in0=rel, scalar=DUP / 2, in1=near, op0=ALU.is_lt, op1=ALU.add))
                    link(nc.vector.tensor_copy(dst_f, dst_i))
                    link(nc.vector.scalar_tensor_tensor(out=dst_f, in0=near, scalar=FAR, in1=dst_f, op0=ALU.mult, op1=ALU.add))
                    dve.wait_ge(product, g + 1)
                    dve.wait_ge(gathered, g * 16 * GATHERS + 16 * GATHERS)
                    if layer == 0:
                        link(nc.vector.tensor_tensor(z, P[:, 0:2, :].rearrange("p b (j c) -> p (b j) c", j=2), rows, ALU.add))
                        for n in range(PARTS):
                            link(nc.vector.tensor_tensor(z, z, parts[:, :, n * 2 * D:(n + 1) * 2 * D], ALU.add))
                        nc.vector.tensor_scalar(e, z, EXP_MAX, None, ALU.min).then_inc(clamped, 1)
                        dve.wait_ge(act_chain, g * 3 + 3)
                        link(nc.vector.tensor_tensor(e[:, :, D:2 * D], e[:, :, D:2 * D], z[:, :, D:2 * D], ALU.max))
                        nc.vector.tensor_tensor(msg, e[:, :, 0:D], e[:, :, D:2 * D], ALU.mult)
                    else:
                        for j in range(TPG):
                            nc.vector.tensor_tensor(msg[:, j, 0:2 * D].rearrange("p (a d) -> p a d", a=2), P[:, j, 0:2 * D].rearrange("p (a d) -> p a d", a=2),
                                                    rows[:, j, 0:D].unsqueeze(1).to_broadcast([128, 2, D]), ALU.mult)
                            nc.vector.tensor_tensor(msg[:, j, 2 * D:3 * D], P[:, j, 2 * D:3 * D], rows[:, j, D:2 * D], ALU.mult)
                    with dve.Fori(0, NT) as b:
                        for j in range(TPG):
                            last = nc.vector.tensor_scalar(oh[:, j, :], iota, dst_f[:, j:j + 1], None, ALU.is_equal)
                        last.then_inc(oh_ready, 1)
                        dve.wait_ge(oh_ready, g * NT + b + 1)
                        nc.vector.tensor_scalar(dst_f, dst_f, -float(NB), None, ALU.add).then_inc(shifted, 1)
                        dve.wait_ge(sums, g * NT + b + 1)
                        dve.wait_ge(shifted, g * NT + b + 1)
                        block_acc = S["acc"][:, 0:accs, bass.ds(b * NB, NB)]
                        nc.vector.tensor_tensor(block_acc, block_acc, P[:, 5:5 + accs, 0:NB], ALU.add).then_inc(added, 1)
                        dve.wait_ge(added, g * NT + b + 1)
                    dve.sem_inc(free, 1)
                if_any(dve, spread)


def node_update(nc, T, S, P, N):
    NT = N // NB
    with ExitStack() as ctx:
        sem = Sems(nc, ctx, "upd")

        def sb(name, shape, dt=F32):
            return ctx.enter_context(nc.sbuf_tensor(f"upd_{name}", shape, dt))

        acc = S["acc"][:, 0, :]
        x = S["acc"][0:NP, 1, 0:NT * NK * D].rearrange("p (t d) -> p t d", d=D)
        stats = S["stats"]
        mean, rstd = sb("mean", [NP, NT * NK]), sb("rstd", [NP, NT * NK])
        tmp = sb("tmp", [NP, 2, NT * NK])
        ag = sb("ag", [D, 2, NB])
        h = sb("h", [NP, 2, NK, D])
        hT = sb("hT", [D, 2, NB])
        room = S["acc"][:, 2, :]
        rows = room[0:NP, 0:2048].rearrange("p (s k c) -> p s k c", s=2, k=NK)
        ROOM = 2048 + 4 * NB
        cols = room[:, 2048:ROOM].rearrange("p (s a c) -> p s a c", s=2, a=2)
        ag_sb, ag_T, x1_ready, st_ready = sem.one("ag_sb"), sem.one("ag_T"), sem.one("x1_ready"), sem.one("st_ready")
        x1_out, h_ready, h_T, h_T_sb = sem.one("x1_out"), sem.one("h_ready"), sem.one("h_T"), sem.one("h_T_sb")
        lin_rows, lin_cols = sem.one("lin_rows"), sem.one("lin_cols")
        rows_ready, cols_ready = sem.one("rows_ready"), sem.one("cols_ready")
        rows_out, cols_out = sem.pair("rows_out"), sem.pair("cols_out")
        norm_v, norm_s = norm_scales(nc, sem, stats, mean, rstd, tmp, S["eps"], NT * NK)
        ident = S["ident"]

        LATE = (NT - 3) * NK * D

        def live(r, c):
            return r is not None or 0 <= c < NT

        def tables_stored(eng):
            for n in range(2):
                eng.wait_ge(rows_out[n], 16 * ((NT + 1 - n) // 2))
                eng.wait_ge(cols_out[n], 16 * ((NT + 1 - n) // 2))
            eng.wait_ge(rows_ready, NT)

        with nc.Block() as block:
            @block.sync
            def _(sp):
                sp.wait_ge(x1_ready, NT)
                sp.dma_start(T["x1"].rearrange("(t p) d -> p t d", p=NP), x).then_inc(x1_out, 16)

                def store(r, c):
                    s = c % 2
                    row = address(sp, r, at(r, c) * NB)
                    col = address(sp, r, at(r, c) * 2 * NB)
                    sp.wait_ge(cols_ready, at(r, c + 1))
                    sp.dma_start(T["x_cols"][:, bass.ds(col, 2 * NB)], cols[:, s].rearrange("p a c -> p (a c)")).then_inc(cols_out[s], 16)
                    sp.wait_ge(rows_ready, at(r, c + 1))
                    sp.dma_start(T["x_rows"][bass.ds(row, NB), :].rearrange("(k p) c -> p k c", p=NP), rows[:, s]).then_inc(rows_out[s], 16)
                run(sp, NT, 2, store)
                sp.wait_ge(x1_out, 16)
                for o in (rows_out, cols_out):
                    sp.wait_ge(o[0], 16 * ((NT + 1) // 2))
                    sp.wait_ge(o[1], 16 * (NT // 2))

            @block.scalar
            def _(act):
                def grab(r, c):
                    s = c % 2
                    if c >= 2:
                        act.wait_ge(ag_T, at(r, c - 1))
                    nc.scalar.copy(ag[:, s, :], acc[:, bass.ds(at(r, c) * NB, NB)]).then_inc(ag_sb, 1)
                run(act, NT, 2, grab)
                norm_s(act)

                def step(r, c):
                    if live(r, c - 2):
                        g, s = c - 2, (c - 2) % 2
                        act.wait_ge(lin_cols, at(r, g + 1))
                        if g >= 2:
                            act.wait_ge(cols_out[s], half(r, g) * 16)
                            act.wait_ge(lin_rows, at(r, g - 1))
                        nc.scalar.activation(cols[:, s, 0, :], P[:, 2, 0:NB], ACT.Silu, bias=S["bcol"][:, 0:1])
                        nc.scalar.activation(cols[:, s, 1, :], P[:, 3, 0:NB], ACT.Silu, bias=S["bcol"][:, 1:2]).then_inc(cols_ready, 1)
                    if live(r, c):
                        s = c % 2
                        act.wait_ge(h_T, at(r, c + 1))
                        if c >= 2:
                            act.wait_ge(lin_cols, at(r, c - 1))
                        nc.scalar.activation(hT[:, s, :], P[:, 4 + s, 0:NB], ACT.Relu).then_inc(h_T_sb, 1)
                run_skewed(act, NT, 3, step)

            @block.vector
            def _(dve):
                def update(r, c):
                    if live(r, c):
                        xs = x[:, bass.ds(at(r, c) * NK, NK), :]
                        dve.wait_ge(ag_T, at(r, c + 1))
                        nc.vector.tensor_tensor(xs, xs, P[0:NP, c % 2, :].rearrange("p (k d) -> p k d", k=NK), ALU.add).then_inc(x1_ready, 1)
                    if live(r, c - 1):
                        dve.wait_ge(x1_ready, at(r, c))
                        for k in range(NK):
                            t = at(r, c - 1) * NK + k
                            last = nc.vector.bn_stats(stats[:, bass.ds(t, 1), :].rearrange("p t c -> p (t c)"),
                                                      x[:, bass.ds(t, 1), :].rearrange("p t c -> p (t c)"))
                        last.then_inc(st_ready, 1)
                run_skewed(dve, NT, 1, update)
                dve.wait_ge(st_ready, NT)
                norm_v(dve)
                def step(r, c):
                    if live(r, c):
                        s = c % 2
                        if c >= 2:
                            dve.wait_ge(h_T, at(r, c - 1))
                        for k in range(NK):
                            t = at(r, c) * NK + k
                            last = nc.vector.tensor_scalar(h[:, s, k, :], x[:, bass.ds(t, 1), :].rearrange("p t c -> p (t c)"),
                                                           mean[:, bass.ds(t, 1)], rstd[:, bass.ds(t, 1)], ALU.subtract, ALU.mult)
                        last.then_inc(h_ready, 1)
                    if live(r, c - 3):
                        g, s = c - 3, (c - 3) % 2
                        dve.wait_ge(lin_rows, at(r, g + 1))
                        if g >= 2:
                            dve.wait_ge(rows_out[s], half(r, g) * 16)
                        nc.vector.tensor_copy(rows[:, s], P[0:NP, 0:2, :].rearrange("p b (k c) -> p (b k) c", k=2)).then_inc(rows_ready, 1)
                run_skewed(dve, NT, 3, step)
                dve.wait_ge(x1_out, 16)
                dve.wait_ge(h_ready, NT)
                nc.vector.memset(S["acc"][:, 1, LATE:], 0.0)
                tables_stored(dve)
                nc.vector.memset(room[:, ROOM // 2:ROOM], 0.0)

            @block.gpsimd
            def _(pool):
                pool.wait_ge(ag_sb, NT)
                nc.gpsimd.memset(acc, 0.0)
                nc.gpsimd.memset(room[:, ROOM:], 0.0)
                pool.wait_ge(x1_out, 16)
                pool.wait_ge(h_ready, NT - 3)
                nc.gpsimd.memset(S["acc"][:, 1, 0:LATE], 0.0)
                tables_stored(pool)
                nc.gpsimd.memset(room[:, 0:ROOM // 2], 0.0)

            @block.tensor
            def _(pe):
                def flip(r, c):
                    s = c % 2
                    pe.wait_ge(ag_sb, at(r, c + 1))
                    if c >= 2:
                        pe.wait_ge(x1_ready, at(r, c - 1))
                    for k in range(NK):
                        last = nc.tensor.transpose(P[0:NP, s, k * D:(k + 1) * D], ag[:, s, k * NP:(k + 1) * NP], ident[:, :])
                    last.then_inc(ag_T, 1)
                run(pe, NT, 2, flip)
                pe.wait_ge(x1_ready, NT)

                def step(r, c):
                    if live(r, c - 2):
                        g, s = c - 2, (c - 2) % 2
                        pe.wait_ge(h_T_sb, at(r, g + 1))
                        if g >= 1:
                            pe.wait_ge(cols_ready, at(r, g))
                        for a in range(2):
                            last = nc.tensor.matmul(P[:, 2 + a, 0:NB], S["w_x"][:, a * D:(a + 1) * D], hT[:, s, :], start=True, stop=True)
                        last.then_inc(lin_cols, 1)
                    if live(r, c - 3):
                        g, s = c - 3, (c - 3) % 2
                        pe.wait_ge(cols_ready, at(r, g + 1))
                        if g >= 1:
                            pe.wait_ge(rows_ready, at(r, g))
                        for k in range(NK):
                            for a in range(2):
                                last = nc.tensor.transpose(P[0:NP, k // 2, (k % 2 * 2 + a) * D:(k % 2 * 2 + a + 1) * D],
                                                           cols[:, s, a, k * NP:(k + 1) * NP], ident[:, :])
                        last.then_inc(lin_rows, 1)
                    if live(r, c):
                        s = c % 2
                        pe.wait_ge(h_ready, at(r, c + 1))
                        if c >= 2:
                            pe.wait_ge(h_T_sb, at(r, c - 1))
                        for k in range(NK):
                            last = nc.tensor.transpose(P[:, 4 + s, k * NP:(k + 1) * NP], h[:, s, k, :], ident[0:NP, 0:NP])
                        last.then_inc(h_T, 1)
                run_skewed(pe, NT, 3, step)


def weighted_edges(nc, T, S, P, N, E):
    G = -(-E // GE)
    with ExitStack() as ctx:
        sem = Sems(nc, ctx, "conv")

        def sb(name, shape, dt=F32):
            return ctx.enter_context(nc.sbuf_tensor(f"conv_{name}", shape, dt))

        acc = S["acc"]
        rows = sb("rows", [128, 4, TPG, 2 * D])
        raw = [sb(f"raw{c}", [128, 2, TPG, FEATS[c]]) for c in range(3)]
        f = sb("f", [128, TPG, FT])
        fT = sb("fT", [FT, 2, TPG, TILE])
        msg = sb("msg", [128, TPG, 3 * D])
        high = sb("high", [128, TPG, 3 * D], F32R)
        low = sb("low", [128, TPG, 3 * D], F32R)
        oh = sb("oh", [128, 2, TPG, WIN], F32R)
        idx = sb("idx", [128, 4, TPG], I32)
        wsum = sb("wsum", [WIN, 3 * D])
        raw_in, rows_in = sem.pair("raw_in"), sem.four("rows_in")
        gathers_begun = sem.one("gathers_begun")
        idx_ready, f_ready, f_T, f_T_sb = sem.one("idx_ready"), sem.one("f_ready"), sem.one("f_T"), sem.one("f_T_sb")
        ew, msg_ready, high_ready, low_ready, sums = (sem.one(x) for x in ("ew", "msg_ready", "high_ready", "low_ready", "sums"))
        oh_ready, added = sem.one("oh_ready"), sem.one("added")
        sums_sb, sums_T = sem.one("sums_sb"), sem.one("sums_T")
        ident = S["ident"]
        FDRAM = (T["edge_attr_24"], T["edge_attr_36"], T["edge_attr_16"])
        start = [sum(FEATS[:c]) for c in range(3)]

        def first_edge(eng, r, c):
            return E - GE if r is None and c == G - 1 else address(eng, r, at(r, c) * GE)

        def live(r, c):
            return r is not None or 0 <= c < G

        with nc.Block() as block:
            @block.sync
            def _(sp):
                def load(r, c):
                    s = c % 2
                    edge = first_edge(sp, r, c)
                    if c >= 2:
                        sp.wait_ge(f_ready, at(r, c - 1))
                    for n in range(3):
                        sp.dma_start(raw[n][:, s], group_rows(FDRAM[n], edge)).then_inc(raw_in[s], 16)
                run(sp, G - 1, 2, load)
                load(None, G - 1)

            @block.gpsimd
            def _(pool):
                def gather(r, c):
                    s = c % 4
                    if c == 0 or c % 2 == G % 2:
                        pool.wait_ge(idx_ready, at(r, 1 if c == 0 and G % 2 else c + 2))
                        if c >= 3:
                            pool.wait_ge(msg_ready, at(r, c - 2) * 2)
                        pool.sem_inc(gathers_begun, 1)
                    for j in range(TPG):
                        nc.gpsimd.indirect_dma_start(rows[:, s, j, :], None, T["x_rows"],
                                                     bass.IndirectOffsetOnAxis(ap=idx[:, c % 4, j:j + 1], axis=0)).then_inc(rows_in[s], 16)
                run(pool, G, 4, gather)

            @block.scalar
            def _(act):
                def indices(r, c):
                    if c >= 4:
                        act.wait_ge(msg_ready, at(r, c - 4) * 2 + 1)
                    nc.scalar.copy(idx[:, c % 4, :], S["src_t"][:, bass.ds(at(r, c), 1), :].rearrange("p g j -> p (g j)")).then_inc(idx_ready, 1)
                indices(None, 0)

                def high_part(r, c, h):
                    g = c - 3
                    act.wait_ge(msg_ready, at(r, g) * 2 + h + 1)
                    if g >= 1:
                        act.wait_ge(sums, at(r, g) * 2 + h - 1)
                    nc.scalar.copy(high[:, 2 * h:2 * h + 2, :], msg[:, 2 * h:2 * h + 2, :]).then_inc(high_ready, 1)

                def step(r, c):
                    if live(r, c - 3):
                        high_part(r, c, 0)
                    if r is not None or c + 1 < G:
                        indices(r, c + 1)
                    if live(r, c - 1):
                        g, s = c - 1, (c - 1) % 2
                        act.wait_ge(f_T, at(r, g + 1))
                        if g >= 2:
                            act.wait_ge(ew, at(r, g - 1) * 2)
                        nc.scalar.copy(fT[:, s], P[0:FT, 4 + s, :].rearrange("p (j e) -> p j e", j=TPG)).then_inc(f_T_sb, 1)
                    if live(r, c - 4):
                        g = c - 4
                        act.wait_ge(sums, at(r, g + 1) * 2)
                        if g >= 1:
                            act.wait_ge(sums_T, at(r, g))
                        nc.scalar.copy(wsum[:, :], P[0:WIN, 6, 0:3 * D]).then_inc(sums_sb, 1)
                    if live(r, c - 3):
                        high_part(r, c, 1)
                    if live(r, c):
                        s = c % 2
                        act.wait_ge(raw_in[s], (half(r, c) + 1) * 48)
                        if c >= 1:
                            act.wait_ge(f_T, at(r, c))
                        for n in range(3):
                            last = nc.scalar.copy(f[:, :, start[n]:start[n] + FEATS[n]], raw[n][:, s])
                        last.then_inc(f_ready, 1)
                run_ahead(act, G, 5, 1, step)

            @block.vector
            def _(dve):
                def products(r, g, h):
                    dve.wait_ge(ew, at(r, g) * 2 + h + 1)
                    if g >= 1:
                        dve.wait_ge(low_ready, at(r, g) * 2 + h - 1)
                    part = slice(2 * h, 2 * h + 2)
                    nc.vector.tensor_tensor(msg[:, part, 0:2 * D].rearrange("p j (a d) -> p j a d", a=2),
                                            P[:, part, 0:2 * D].rearrange("p j (a d) -> p j a d", a=2),
                                            rows[:, g % 4, part, 0:D].unsqueeze(2).to_broadcast([128, 2, 2, D]), ALU.mult)
                    nc.vector.tensor_tensor(msg[:, part, 2 * D:3 * D], P[:, part, 2 * D:3 * D], rows[:, g % 4, part, D:2 * D],
                                            ALU.mult).then_inc(msg_ready, 1)

                def low_part(r, g, h):
                    part = slice(2 * h, 2 * h + 2)
                    dve.wait_ge(high_ready, at(r, g) * 2 + h + 1)
                    if g >= 1:
                        dve.wait_ge(sums, at(r, g) * 2 + h - 1)
                    nc.vector.tensor_tensor(low[:, part, :], msg[:, part, :], high[:, part, :].bitcast(F32), ALU.subtract).then_inc(low_ready, 1)

                def step(r, c):
                    if live(r, c - 3):
                        g, s = c - 3, (c - 3) % 2
                        if g >= 2:
                            dve.wait_ge(sums, at(r, g - 1) * 2)
                        nc.vector.tensor_tensor(oh[:, s], S["iota"][:, 0:WIN].unsqueeze(1).to_broadcast([128, TPG, WIN]),
                                                S["rel_t"][:, bass.ds(at(r, g), 1), :].rearrange("p g j -> p (g j)").unsqueeze(2).to_broadcast([128, TPG, WIN]),
                                                ALU.is_equal).then_inc(oh_ready, 1)
                        dve.wait_ge(rows_in[g % 4], (quarter(r, g) + 1) * 16 * TPG)
                        products(r, g, 0)
                    if live(r, c - 4):
                        low_part(r, c - 4, 1)
                    if live(r, c - 3):
                        products(r, c - 3, 1)
                    if live(r, c - 5):
                        g = c - 5
                        base = dve.value_load(S["base_i"][0:1, bass.ds(at(r, g), 1)], min_val=0, max_val=N - 1)
                        dve.wait_ge(sums_T, at(r, g + 1))
                        if g >= 1:
                            dve.wait_ge(added, at(r, g))
                        nc.vector.tensor_tensor(acc[:, :, bass.ds(base, WIN)], acc[:, :, bass.ds(base, WIN)],
                                                P[:, 7, 0:3 * WIN].rearrange("p (a w) -> p a w", a=3), ALU.add).then_inc(added, 1)
                    if live(r, c - 3):
                        low_part(r, c - 3, 0)
                run_skewed(dve, G, 5, step)

            @block.tensor
            def _(pe):
                def weights(r, g, h):
                    if h == 0:
                        pe.wait_ge(f_T_sb, at(r, g + 1))
                    if g >= 1:
                        pe.wait_ge(msg_ready, at(r, g) * 2 + h - 1)
                    for j in (2 * h, 2 * h + 1):
                        last = nc.tensor.matmul(P[:, j, 0:3 * D], fT[:, g % 2, j, :], S["w_edge"][:, :], start=True, stop=True)
                    last.then_inc(ew, 1)

                def window_sums(r, g, h):
                    s = g % 2
                    pe.wait_ge(low_ready, at(r, g) * 2 + h + 1)
                    if h == 0:
                        pe.wait_ge(oh_ready, at(r, g + 1))
                        if g >= 1:
                            pe.wait_ge(sums_sb, at(r, g))
                    for j in (2 * h, 2 * h + 1):
                        nc.tensor.matmul(P[0:WIN, 6, 0:3 * D], oh[:, s, j, :], high[:, j, :], start=j == 0, stop=False)
                        last = nc.tensor.matmul(P[0:WIN, 6, 0:3 * D], oh[:, s, j, :], low[:, j, :], start=False, stop=j == TPG - 1)
                    last.then_inc(sums, 1)

                def step(r, c):
                    if live(r, c - 2):
                        weights(r, c - 2, 0)
                    if live(r, c - 1):
                        g, s = c - 1, (c - 1) % 2
                        pe.wait_ge(f_ready, at(r, g + 1))
                        if g >= 2:
                            pe.wait_ge(f_T_sb, at(r, g - 1))
                        for j in range(TPG):
                            last = nc.tensor.transpose(P[0:FT, 4 + s, j * TILE:(j + 1) * TILE], f[:, j, :], ident[:, :])
                        last.then_inc(f_T, 1)
                    if live(r, c - 4):
                        window_sums(r, c - 4, 1)
                    if live(r, c - 2):
                        weights(r, c - 2, 1)
                    if live(r, c - 4):
                        g = c - 4
                        pe.wait_ge(sums_sb, at(r, g + 1))
                        if g >= 1:
                            pe.wait_ge(added, at(r, g))
                    if live(r, c - 3):
                        window_sums(r, c - 3, 0)
                    if live(r, c - 4):
                        for a in range(3):
                            last = nc.tensor.transpose(P[:, 7, a * WIN:(a + 1) * WIN], wsum[:, a * D:(a + 1) * D], ident[0:WIN, 0:WIN])
                        last.then_inc(sums_T, 1)
                run_skewed(pe, G, 5, step)


def node_output(nc, T, S, P, N):
    NT = N // NB
    with ExitStack() as ctx:
        sem = Sems(nc, ctx, "out")

        def sb(name, shape, dt=F32):
            return ctx.enter_context(nc.sbuf_tensor(f"out_{name}", shape, dt))

        acc = S["acc"]
        xc = sb("xc", [D, 2, 2, NB])
        x1 = sb("x1", [NP, 2, NK, D])
        hc = sb("hc", [D, 2, 3, NB])
        o = sb("o", [D, 2, NB])
        w_out = sb("w_out", [D, 7, D])
        w_in = sem.one("w_in")
        xc_in, x1_in, out_done = sem.pair("xc_in"), sem.pair("x1_in"), sem.pair("out_done")
        y, h_act, h_part, h_sum, y3, o_ready, o_T, res = (sem.one(x) for x in ("y", "h_act", "h_part", "h_sum", "y3", "o_ready", "o_T", "res"))
        ident = S["ident"]
        XC = (0, 0, 1)

        def live(r, c):
            return r is not None or 0 <= c < NT

        with nc.Block() as block:
            @block.sync
            def _(sp):
                def load(r, c):
                    if live(r, c):
                        load_cols(r, c)
                    if live(r, c - 2):
                        load_x1(r, c - 2)

                def load_cols(r, c):
                    s = c % 2
                    col = address(sp, r, at(r, c) * 2 * NB)
                    if c >= 2:
                        sp.wait_ge(y, at(r, c - 1) * 3)
                    sp.dma_start(xc[:, s].rearrange("p a c -> p (a c)"), T["x_cols"][:, bass.ds(col, 2 * NB)]).then_inc(xc_in[s], 16)

                def load_x1(r, c):
                    s = c % 2
                    row = address(sp, r, at(r, c) * NB)
                    if c >= 2:
                        sp.wait_ge(out_done[s], half(r, c) * 16)
                    sp.dma_start(x1[:, s], T["x1"][bass.ds(row, NB), :].rearrange("(k p) d -> p k d", p=NP)).then_inc(x1_in[s], 16)
                run_skewed(sp, NT, 2, load)

            @block.gpsimd
            def _(pool):
                def store(r, c):
                    s = c % 2
                    pool.wait_ge(res, at(r, c + 1))
                    pool.dma_start(T["out"][bass.ds(at(r, c) * NB, NB), :].rearrange("(k p) d -> p k d", p=NP), x1[:, s]).then_inc(out_done[s], 16)
                run(pool, NT, 2, store)
                pool.wait_ge(out_done[0], 16 * ((NT + 1) // 2))
                pool.wait_ge(out_done[1], 16 * (NT // 2))

            @block.tensor
            def _(pe):
                pe.wait_ge(w_in, 16)

                def step(r, c):
                    if live(r, c):
                        s = c % 2
                        pe.wait_ge(xc_in[s], (half(r, c) + 1) * 16)
                        for a in range(3):
                            if c >= 1:
                                pe.wait_ge(h_act, at(r, c) * 3 + a - 2)
                            nc.tensor.matmul(P[:, a, 0:NB], w_out[:, a, :], acc[:, a, bass.ds(at(r, c) * NB, NB)], start=True, stop=False)
                            nc.tensor.matmul(P[:, a, 0:NB], w_out[:, 3 + a, :], xc[:, s, XC[a], :], start=False, stop=True).then_inc(y, 1)
                    if live(r, c - 1):
                        g, s = c - 1, (c - 1) % 2
                        pe.wait_ge(h_sum, at(r, g + 1))
                        if g >= 2:
                            pe.wait_ge(o_ready, at(r, g - 1))
                        nc.tensor.matmul(P[:, 3 + s, 0:NB], w_out[:, 6, :], hc[:, s, 0, :], start=True, stop=True).then_inc(y3, 1)
                    if live(r, c - 2):
                        g, s = c - 2, (c - 2) % 2
                        pe.wait_ge(o_ready, at(r, g + 1))
                        if g >= 2:
                            pe.wait_ge(res, at(r, g - 1))
                        for k in range(NK):
                            last = nc.tensor.transpose(P[0:NP, 5 + s, k * D:(k + 1) * D], o[:, s, k * NP:(k + 1) * NP], ident[:, :])
                        last.then_inc(o_T, 1)
                run_skewed(pe, NT, 3, step)

            @block.scalar
            def _(act):
                act.dma_start(w_out[:, :, :].rearrange("p a d -> p (a d)"), T["w_out"]).then_inc(w_in, 16)

                def step(r, c):
                    if live(r, c):
                        s = c % 2
                        if c >= 2:
                            act.wait_ge(y3, at(r, c - 1))
                        for a in range(3):
                            act.wait_ge(y, at(r, c) * 3 + a + 1)
                            nc.scalar.activation(hc[:, s, a, :], P[:, a, 0:NB], ACT.Silu, bias=S["b_h"][:, a:a + 1]).then_inc(h_act, 1)
                    if live(r, c - 1):
                        g, s = c - 1, (c - 1) % 2
                        act.wait_ge(y3, at(r, g + 1))
                        if g >= 2:
                            act.wait_ge(o_T, at(r, g - 1))
                        nc.scalar.activation(o[:, s, :], P[:, 3 + s, 0:NB], ACT.Silu, bias=S["bcol"][:, 2:3]).then_inc(o_ready, 1)
                run_skewed(act, NT, 3, step)

            @block.vector
            def _(dve):
                def step(r, c):
                    if live(r, c - 3):
                        g, s = c - 3, (c - 3) % 2
                        dve.wait_ge(o_T, at(r, g + 1))
                        dve.wait_ge(x1_in[s], (half(r, g) + 1) * 16)
                        nc.vector.tensor_tensor(x1[:, s], P[0:NP, 5 + s, :].rearrange("p (k d) -> p k d", k=NK), x1[:, s], ALU.add).then_inc(res, 1)
                    if live(r, c):
                        s = c % 2
                        dve.wait_ge(h_act, at(r, c) * 3 + 2)
                        nc.vector.tensor_tensor(hc[:, s, 0, :], hc[:, s, 0, :], hc[:, s, 1, :], ALU.add).then_inc(h_part, 1)
                        dve.wait_ge(h_part, at(r, c + 1))
                        dve.wait_ge(h_act, at(r, c) * 3 + 3)
                        nc.vector.tensor_tensor(hc[:, s, 0, :], hc[:, s, 0, :], hc[:, s, 2, :], ALU.add).then_inc(h_sum, 1)
                run_skewed(dve, NT, 3, step)


def gnn_two_layers(nc, T, N, E):
    G = -(-E // GE)
    for name, shape, dt in (("a_rows", [N + WIN, PARTS * 2 * D], BF16), ("b_rows", [N, 2 * D], F32), ("x_rows", [N, 2 * D], F32),
                            ("x_cols", [D, 2 * N], F32), ("x1", [N, D], F32), ("rel_rows", [G, GE], BF16), ("w_out", [D, 7 * D], F32)):
        T[name] = nc.dram_tensor(f"scratch_{name}", shape, dt, kind="Internal").ap()
    with ExitStack() as ctx:
        def sb(name, shape, dt=F32):
            return ctx.enter_context(nc.sbuf_tensor(name, shape, dt))

        P = ctx.enter_context(nc.psum_tensor("P", [128, 8, 512], F32))
        S = {
            "acc": sb("acc", [D, 3, max(N + WIN, N // NP * D)]),
            "rel_t": sb("rel_t", [TILE, G, TPG], BF16), "src_t": sb("src_t", [TILE, G, TPG]),
            "base_i": sb("base_i", [1, G], I32), "base_f": sb("base_f", [128, 4]), "far_i": sb("far_i", [1, 1], I32),
            "ident": sb("ident", [128, 128]), "iota": sb("iota", [128, WIN]), "wrow": sb("wrow", [WROWS, 1]),
            "ones": sb("ones", [128, 1]), "eps": sb("eps", [128, 1]),
            "w_edge": sb("w_edge", [FT, 3 * D]),
            "b_h": sb("b_h", [D, 3]), "bcol": sb("bcol", [D, 3]),
        }
        with ExitStack() as early:
            for name, shape in (("w_ab", [D, 4 * D]), ("w_e", [D, 2 * D]), ("w_x", [D, 2 * D]), ("bias_ab", [NP, 2 * D]), ("w_out", [D, 7 * D])):
                S[name] = early.enter_context(nc.sbuf_tensor(name, shape, F32))
            S["stats"] = early.enter_context(nc.sbuf_tensor("stats", [NP, N // NP, 6], F32))
            constants_and_weights(nc, T, S, P, N, E)
            node_tables(nc, T, S, P, N)
            gated_edges(nc, T, S, P, N, E)
            far_edges(nc, T, S, P, N, E, 0)
            node_update(nc, T, S, P, N)
        weighted_edges(nc, T, S, P, N, E)
        far_edges(nc, T, S, P, N, E, 1)
        node_output(nc, T, S, P, N)


def shape_constants(N, E):
    G = -(-E // GE)
    dup = np.zeros((128, GE), np.float32)
    dup[(G - 1) % 128, 0:GE * G - E] = 1.0
    return {
        "c_ident": np.eye(128, dtype=np.float32),
        "c_iota": np.arange(NB, dtype=np.float32),
        "c_wrow": (np.arange(WROWS) // PARTS).astype(np.float32)[:, None],
        "c_dup": dup,
    }


def kernel(**inputs):
    import concourse.bacc as bacc
    from concourse.bass_utils import run_bass_kernel_spmd

    nc = bacc.Bacc("TRN2", target_bir_lowering=False, num_devices=1)
    arrays = {k: np.ascontiguousarray(v) for k, v in inputs.items()}
    N, E = arrays["x"].shape[0], arrays["src"].shape[0]
    arrays.update(shape_constants(N, E))
    T = {k: nc.dram_tensor(f"in_{k}", list(a.shape), mybir.dt.from_np(a.dtype), kind="ExternalInput").ap() for k, a in arrays.items()}
    T["out"] = nc.dram_tensor("out_x", [N, D], F32, kind="ExternalOutput").ap()
    gnn_two_layers(nc, T, N, E)
    r = run_bass_kernel_spmd(nc, [{f"in_{k}": a for k, a in arrays.items()}], core_ids=[0])
    return r.results[0]["out_x"]
```
